# Optimizing a Trainium2 kernel written in Bass

```python
import numpy as np
import jax
import jax.numpy as jnp

def _softmax(x, axis=-1):
    return jax.nn.softmax(x, axis=axis)

def _gelu(x):
    return jax.nn.gelu(x, approximate=True)

def _silu(x):
    return jax.nn.silu(x)

def _sigmoid(x):
    return jax.nn.sigmoid(x)

def _layernorm(x, axis=-1, eps=1e-05):
    m = jnp.mean(x, axis=axis, keepdims=True)
    v = jnp.var(x, axis=axis, keepdims=True)
    return (x - m) / jnp.sqrt(v + eps)

def _scatter_add(tgt, idx, src, axis=0):
    return tgt.at[idx].add(src)

def _segment_sum(src, seg, n):
    return jax.ops.segment_sum(src, seg, n)
kernel_name = 'mk_conv_preact_d2_conv_nchw384_r4_25cd39'

def setup_inputs(seed: int=0):
    np.random.seed(seed)
    _w = jnp.asarray

    def _rec_inputs():
        import jax
        import jax.numpy as jnp
        _gk = jax.random.key(seed)
        x = -0.0002221 + 1 * jax.random.normal(jax.random.fold_in(_gk, 1), (16, 96, 16, 16), jnp.float32)
        return x
    x = _rec_inputs()

    def _L0_conv_setup():
        import jax, jax.numpy as jnp
        import numpy as np
        from jax import lax
        NUM_HEADS = 8
        EPS = 1e-12

        def _l2norm(t):
            n = jnp.sqrt(jnp.sum(t * t, axis=-1, keepdims=True))
            return t / jnp.maximum(n, EPS)
        key = jax.random.key(seed)
        k1, k2, k3, k4 = jax.random.split(key, 4)
        b, c, h, w = (16, 96, 16, 16)
        x = jax.random.normal(k1, (b, c, h, w), dtype=jnp.float32)
        w_qkv = jax.random.normal(k2, (3 * c, c), dtype=jnp.float32) * (1.0 / np.sqrt(c))
        w_dw = jax.random.normal(k3, (3 * c, 1, 3, 3), dtype=jnp.float32) * (1.0 / 3.0)
        w_proj = jax.random.normal(k4, (c, c), dtype=jnp.float32) * (1.0 / np.sqrt(c))
        temperature = jnp.ones((1, NUM_HEADS, 1, 1), dtype=jnp.float32)
        return {'x': x, 'w_qkv': w_qkv, 'w_dw': w_dw, 'w_proj': w_proj, 'temperature': temperature}
    _L0_conv_all = _L0_conv_setup()
    _L0_conv_in = {k: v for k, v in _L0_conv_all.items() if k in ('w_qkv', 'w_dw', 'w_proj', 'temperature')}
    del _L0_conv_all

    def _L1_conv_setup():
        import jax, jax.numpy as jnp
        import numpy as np
        B, C, H, W = (32, 96, 28, 28)
        E, HID, K = (4, 96, 2)
        key = jax.random.key(seed)
        ks = jax.random.split(key, 5)
        x = jax.random.normal(ks[0], (B, C, H, W), jnp.float32)
        gate_w = jax.random.normal(ks[1], (C, E), jnp.float32) * 0.02
        gate_b = jnp.zeros((E,), jnp.float32)
        w1 = jax.random.normal(ks[2], (E, HID, C), jnp.float32) * 0.02
        b1 = jnp.zeros((E, HID), jnp.float32)
        w2 = jax.random.normal(ks[3], (E, C, HID), jnp.float32) * 0.02
        b2 = jnp.zeros((E, C), jnp.float32)
        return {'x': x, 'gate_w': gate_w, 'gate_b': gate_b, 'w1': w1, 'b1': b1, 'w2': w2, 'b2': b2}
    _L1_conv_all = _L1_conv_setup()
    _L1_conv_in = {k: v for k, v in _L1_conv_all.items() if k in ('gate_w', 'gate_b', 'w1', 'b1', 'w2', 'b2')}
    del _L1_conv_all
    return {'x': x, 'L0_conv_w_qkv': _L0_conv_in['w_qkv'], 'L0_conv_w_dw': _L0_conv_in['w_dw'], 'L0_conv_w_proj': _L0_conv_in['w_proj'], 'L0_conv_temperature': _L0_conv_in['temperature'], 'L1_conv_gate_w': _L1_conv_in['gate_w'], 'L1_conv_gate_b': _L1_conv_in['gate_b'], 'L1_conv_w1': _L1_conv_in['w1'], 'L1_conv_b1': _L1_conv_in['b1'], 'L1_conv_w2': _L1_conv_in['w2'], 'L1_conv_b2': _L1_conv_in['b2']}

def reference(x, L0_conv_w_qkv, L0_conv_w_dw, L0_conv_w_proj, L0_conv_temperature, L1_conv_gate_w, L1_conv_gate_b, L1_conv_w1, L1_conv_b1, L1_conv_w2, L1_conv_b2):
    import jax
    import jax.numpy as jnp

    def _L0_conv_ref(x, w_qkv, w_dw, w_proj, temperature):
        import jax, jax.numpy as jnp
        import numpy as np
        from jax import lax
        NUM_HEADS = 8
        EPS = 1e-12

        def _l2norm(t):
            n = jnp.sqrt(jnp.sum(t * t, axis=-1, keepdims=True))
            return t / jnp.maximum(n, EPS)
        b, c, h, w = x.shape
        hw = h * w
        d = c // NUM_HEADS
        qkv = jnp.einsum('bchw,oc->bohw', x, w_qkv)
        qkv = lax.conv_general_dilated(qkv, w_dw, window_strides=(1, 1), padding='SAME', feature_group_count=3 * c, dimension_numbers=('NCHW', 'OIHW', 'NCHW'))
        q, k, v = jnp.split(qkv, 3, axis=1)
        q = q.reshape(b, NUM_HEADS, d, hw)
        k = k.reshape(b, NUM_HEADS, d, hw)
        v = v.reshape(b, NUM_HEADS, d, hw)
        q = _l2norm(q)
        k = _l2norm(k)
        scores = jnp.einsum('bhdn,bhen->bhde', q, k) * temperature
        attn = jax.nn.softmax(scores, axis=-1)
        out = jnp.einsum('bhde,bhen->bhdn', attn, v).reshape(b, c, h, w)
        out = jnp.einsum('bchw,oc->bohw', out, w_proj)
        return out

    def _L1_conv_ref(x, gate_w, gate_b, w1, b1, w2, b2):
        import jax, jax.numpy as jnp
        import numpy as np
        B, C, H, W = (32, 96, 28, 28)
        E, HID, K = (4, 96, 2)
        b, c, h, w = x.shape
        e = gate_b.shape[0]
        x_flat = x.transpose(0, 2, 3, 1).reshape(-1, c)
        scores = jax.nn.softmax(x_flat @ gate_w + gate_b, -1)
        top_v, top_i = jax.lax.top_k(scores, K)
        top_w = jax.nn.softmax(top_v, -1)
        wmap = top_w.T.reshape(K, b, h, w)
        present = (top_i[:, :, None] == jnp.arange(e)[None, None, :]).any(0)
        coef = jnp.einsum('ke,kbhw->ebhw', present.astype(x.dtype), wmap)
        hdn = jax.nn.relu(jnp.einsum('bchw,edc->ebdhw', x, w1) + b1[:, None, :, None, None])
        y = jnp.einsum('ebdhw,eod->ebohw', hdn, w2) + b2[:, None, :, None, None]
        out = jnp.einsum('ebohw,ebhw->bohw', y, coef)
        return out

    def _gn(v, G=32, eps=1e-05):
        B_, C_, H_, W_ = v.shape
        g = v.reshape(B_, G, C_ // G, H_, W_)
        m = jnp.mean(g, axis=(2, 3, 4), keepdims=True)
        s = jnp.var(g, axis=(2, 3, 4), keepdims=True)
        return ((g - m) / jnp.sqrt(s + eps)).reshape(v.shape)

    def _ln_c(v, eps=1e-06):
        m = jnp.mean(v, axis=1, keepdims=True)
        s = jnp.var(v, axis=1, keepdims=True)
        return (v - m) / jnp.sqrt(s + eps)

    def _ln_t(v, eps=1e-05):
        m = jnp.mean(v, axis=-1, keepdims=True)
        s = jnp.var(v, axis=-1, keepdims=True)
        return (v - m) / jnp.sqrt(s + eps)

    def _to_tokens(v):
        B_, C_, H_, W_ = v.shape
        return v.reshape(B_, C_, H_ * W_).transpose(0, 2, 1)

    def _from_tokens(t, like):
        B_, C_, H_, W_ = like.shape
        return t.transpose(0, 2, 1).reshape(B_, C_, H_, W_)
    x = x + _L0_conv_ref(_gn(x), L0_conv_w_qkv, L0_conv_w_dw, L0_conv_w_proj, L0_conv_temperature)
    x = x + _L1_conv_ref(_gn(x), L1_conv_gate_w, L1_conv_gate_b, L1_conv_w1, L1_conv_b1, L1_conv_w2, L1_conv_b2)
    return x

_drawn_inputs = setup_inputs


def setup_inputs(seed=0):
    import zlib

    import numpy as np

    out = dict(_drawn_inputs(seed))
    spreads = {'L0_conv_temperature': (1.0, 0.6),
     'L1_conv_gate_b': (0.0, 0.8),
     'L1_conv_b1': (0.0, 0.335),
     'L1_conv_b2': (0.0, 0.1)}
    factors = {'L1_conv_gate_w': 8.0}
    for name, (base, spread) in spreads.items():
        noise = np.random.default_rng([zlib.crc32(name.encode()), seed]).standard_normal(out[name].shape)
        drawn = base * np.exp(spread * noise) if base else spread * noise
        out[name] = jnp.asarray(drawn.astype(out[name].dtype))
    for name, factor in factors.items():
        out[name] = (out[name] * factor).astype(out[name].dtype)
    return out
```

```python
from contextlib import ExitStack

import concourse.bass as bass
from concourse import mybir

ALU = mybir.AluOpType
ACT = mybir.ActivationFunctionType
AX = mybir.AxisListType
F32 = mybir.dt.float32
F16 = mybir.dt.float16
BF16 = mybir.dt.bfloat16

B, C, H, W = 16, 96, 16, 16
HW = H * W
PAIRS = B // 2
T = 2 * HW
TILES = T // 128
TAPS = 9
HEADS = 8
D = C // HEADS
GROUP = C // 32
EXPERTS = 4
ED = EXPERTS * C
MT = ED // 128
QK = 2 * C
GN_EPS = 1e-5
L2_EPS = 1e-12
X_SCALE = 16.0
W_SCALE = 16.0
TINY = 1e-20
TOP_DIFF = 14
URANK = 6
U = 2 * URANK
VP = W + 1
VROWS = 2 * H + 1

CONSTS = [("ident", 128), ("avg", C), ("dev", C), ("head", C), ("slot", D), ("tri", 16),
          ("sel", 2), ("part", 3)]
CONST_AT = {}
_at = 0
for _n, _w in CONSTS:
    CONST_AT[_n] = (_at, _at + _w)
    _at += _w
CONST_W = _at


def build(nc, x, w_qkv, w_dw, w_proj, temperature, gate_w, gate_b, w1, b1, w2, b2, consts, out):
    ctx = ExitStack()
    with ctx:
        def sb(name, shape, dt=F32):
            return ctx.enter_context(nc.sbuf_tensor(name, shape, dt))

        def sem(name):
            return ctx.enter_context(nc.semaphore(name))

        cst = sb("cst", [128, CONST_W])

        def const(name, parts):
            a, b = CONST_AT[name]
            return cst[0:parts, a:b]

        wqkv_sb = sb("wqkv_sb", [C, 3, C])
        wdw_sb = sb("wdw_sb", [C, 3, TAPS])
        wdw_all = sb("wdw_all", [C, QK * TAPS])
        wproj_sb = sb("wproj_sb", [C, C])
        temp_sb = sb("temp_sb", [C, 1])
        gate_w_sb = sb("gate_w_sb", [C, EXPERTS])
        gate_b_sb = sb("gate_b_sb", [128, EXPERTS])
        w1_sb = sb("w1_sb", [128, MT, C])
        b1_sb = sb("b1_sb", [128, MT])
        w2_sb = sb("w2_sb", [C, ED])
        b2_sb = sb("b2_sb", [EXPERTS, C])
        ones = sb("ones", [128, 128])
        minus_half = sb("minus_half", [C, 26])
        max_w = sb("max_w", [C, 3])
        max_dw = sb("max_dw", [C, 3])
        row_max = sb("row_max", [C, 3])
        row_scale = sb("row_scale", [C, 3])
        wqkv_scaled = sb("wqkv_scaled", [C, 3, C])
        floors = sb("floors", [C, 2])
        k_floor_diag = sb("k_floor_diag", [C, D])
        k_floor = sb("k_floor", [C, D])
        v_taps = sb("v_taps", [C, TAPS])
        wc = sb("wc", [C, TAPS, QK])
        wc_hi = sb("wc_hi", [C, TAPS, QK], F16)
        wc_lo = sb("wc_lo", [C, TAPS, QK], F16)
        wv_hi = sb("wv_hi", [C, C], F16)
        wv_lo = sb("wv_lo", [C, C], F16)
        wprojT = sb("wprojT", [C, C])
        w1T = sb("w1T", [C, MT, 128])
        w2T = sb("w2T", [128, MT, C])

        x_sb = sb("x_sb", [C, PAIRS, T])
        stats = sb("stats", [C, 4, 6])
        mv = sb("mv", [C, 4, 2])
        dev2 = sb("dev2", [C, 4])
        var_dev = sb("var_dev", [C, 4])
        var_eps = sb("var_eps", [C, 4])
        rstd = sb("rstd", [C, 4])
        shift = sb("shift", [C, 4])
        xs = [sb(f"xs{p}", [C, T]) for p in range(2)]
        x_hi = [sb(f"x_hi{p}", [C, 3, 2, H + 2, W], F16) for p in range(2)]
        x_lo = [sb(f"x_lo{p}", [C, 3, 2, H + 2, W], F16) for p in range(2)]
        v_grid = sb("v_grid", [C, (VROWS + 2) * VP + 2])
        v_acc = [sb(f"v_acc{p}", [C, VROWS, W]) for p in range(2)]
        qk_sb = sb("qk_sb", [128, TILES, QK])
        qk_sq = sb("qk_sq", [128, TILES, QK])
        masked = sb("masked", [C, 4, C])
        picked = sb("picked", [C, 4, D])
        norm2 = sb("norm2", [C, 2 * D + 2])
        rnorm = sb("rnorm", [C, 2 * D + 2])
        q_fac = sb("q_fac", [C, 2])
        sc_k = sb("sc_k", [C, 2, D])
        sc_qk = sb("sc_qk", [C, 2, D])
        sc_max = sb("sc_max", [C, 2])
        sc_in = sb("sc_in", [C, 2, D])
        sc_exp = sb("sc_exp", [C, 2, D])
        sc_sum = sb("sc_sum", [C, 2])
        sc_rec = sb("sc_rec", [C, 2])
        probs = sb("probs", [C, 2, D])
        attn = sb("attn", [C, 2, C])
        mix_sb = sb("mix_sb", [C, 2, C])
        xn2 = sb("xn2", [C, T])
        hidden = sb("hidden", [128, PAIRS, MT, T])
        logits = sb("logits", [128, PAIRS, TILES, EXPERTS])
        NT = PAIRS * TILES
        g_max = sb("g_max", [128, NT])
        g_in = sb("g_in", [128, NT, EXPERTS])
        g_exp = sb("g_exp", [128, NT, EXPERTS])
        g_sum = sb("g_sum", [128, NT])
        g_rec = sb("g_rec", [128, NT])
        g_prob = sb("g_prob", [128, NT, EXPERTS])
        beats = sb("beats", [128, NT, EXPERTS, EXPERTS])
        ties = sb("ties", [128, NT, 16])
        beaten = sb("beaten", [128, NT, 16])
        rank = sb("rank", [128, NT, EXPERTS])
        chosen = sb("chosen", [128, 2, NT, EXPERTS])
        present = sb("present", [128, 2, EXPERTS])
        top_all = sb("top_all", [128, 2, NT, EXPERTS])
        top = sb("top", [128, 2, NT])
        top_diff = sb("top_diff", [128, NT])
        top_exp = sb("top_exp", [128, NT])
        top_den = sb("top_den", [128, NT])
        top_w = sb("top_w", [128, 2, NT])
        tw_hi = sb("tw_hi", [128, 2, NT], BF16)
        tw_rest = sb("tw_rest", [128, 2, NT])
        tw_mid = sb("tw_mid", [128, 2, NT], BF16)
        tw_lo = sb("tw_lo", [128, 2, NT], BF16)
        u_tok = sb("u_tok", [128, NT, U], BF16)
        ident_bf = sb("ident_bf", [128, 128], BF16)
        u_sb = sb("u_sb", [U, B * HW], BF16)
        on_rows = sb("on_rows", [U, 2 * EXPERTS])
        on_cols = sb("on_cols", [EXPERTS, U])
        spread0 = sb("spread0", [U, EXPERTS, C])
        spread = sb("spread", [U, ED], BF16)
        bias_hi = sb("bias_hi", [U, C], BF16)
        bias_rest = sb("bias_rest", [U, C])
        bias_mid = sb("bias_mid", [U, C], BF16)
        bias_lo = sb("bias_lo", [U, C], BF16)
        bias_a = sb("bias_a", [U, C])
        bias_b = sb("bias_b", [U, C])
        bias_u = sb("bias_u", [U, C], BF16)
        h_mixed = [sb(f"h_mixed{p}", [128, MT, T]) for p in range(2)]
        out_sb = [sb(f"out_sb{p}", [C, T]) for p in range(2)]

        bank = [ctx.enter_context(nc.psum_tensor(f"bank{n}", [128, 512], F32)) for n in range(8)]
        qk_ps = bank[0:2]
        v_ps = bank[2]
        sc_ps = bank[3]
        small_ps = bank[4]
        out_ps = bank[5]
        hid_ps = bank[6:8]
        MEAN, DEVI, VAR, MIX, LOGIT = 0, 4, 8, 16, 16 + QK

        in_w = sem("in_w")
        in_dw = sem("in_dw")
        in_late = sem("in_late")
        in_x = [sem(f"in_x{p}") for p in range(2)]
        ones_set = sem("ones_set")
        pads_set = sem("pads_set")
        prep = sem("prep")
        passed = sem("passed")
        wT_ready = sem("wT_ready")
        wc_full = sem("wc_full")
        wc_hi_set = sem("wc_hi_set")
        wc_lo_set = sem("wc_lo_set")
        wv_set = sem("wv_set")
        floors_set = sem("floors_set")
        kfl_ready = sem("kfl_ready")
        kfl_set = sem("kfl_set")
        late_T = sem("late_T")
        late_set = sem("late_set")
        stats_done = sem("stats_done")
        mv_ready = sem("mv_ready")
        mean_ready = sem("mean_ready")
        dev_ready = sem("dev_ready")
        vd_ready = sem("vd_ready")
        var_ready = sem("var_ready")
        eps_ready = sem("eps_ready")
        rstd_ready = sem("rstd_ready")
        norm_done = sem("norm_done")
        xs_ready = sem("xs_ready")
        hi_mid = sem("hi_mid")
        hi_ready = sem("hi_ready")
        lo_mid = sem("lo_mid")
        lo_ready = sem("lo_ready")
        v_ready = sem("v_ready")
        v_taken = sem("v_taken")
        v_init = sem("v_init")
        tap_done = sem("tap_done")
        tile_done = sem("tile_done")
        qk_taken = sem("qk_taken")
        gram_done = sem("gram_done")
        gram_taken = sem("gram_taken")
        norm2_ready = sem("norm2_ready")
        rnorm_ready = sem("rnorm_ready")
        sm_step = sem("sm_step")
        sc_ready = sem("sc_ready")
        exp_ready = sem("exp_ready")
        attn_ready = sem("attn_ready")
        mix_done = sem("mix_done")
        mix_ready = sem("mix_ready")
        out_done = sem("out_done")
        x1_done = sem("x1_done")
        xn2_ready = sem("xn2_ready")
        gate_done = sem("gate_done")
        logit_free = sem("logit_free")
        hid_done = sem("hid_done")
        hid_free = sem("hid_free")
        g_step = sem("g_step")
        g_exp_ready = sem("g_exp_ready")
        top_exp_ready = sem("top_exp_ready")
        present_ready = sem("present_ready")
        count_done = sem("count_done")
        on_cols_ready = sem("on_cols_ready")
        bias_done = sem("bias_done")
        spread_ready = sem("spread_ready")
        bias_ready = sem("bias_ready")
        u_ready = sem("u_ready")
        uT_done = sem("uT_done")
        u_taken = sem("u_taken")
        coef_done = sem("coef_done")
        mixed_done = sem("mixed_done")
        y_done = sem("y_done")
        y_taken = sem("y_taken")
        stored = [sem(f"stored{p}") for p in range(2)]

        x_dram = x.rearrange("(i b) c h w -> i c b (h w)", b=2)
        out_dram = out.rearrange("(i b) c h w -> i c b (h w)", b=2)

        def wait(eng, s, value):
            if not isinstance(value, int) or value > 0:
                eng.wait_ge(s, value)

        def wait_apart(eng, s, value):
            wait(eng, s, value)
            if not isinstance(value, int):
                eng.sem_inc(passed, 1)

        def x_landed(pair, parity):
            return 8 * (pair - parity) + 16

        def inner(t, dx):
            return t[:, dx, :, 1:H + 1, :]

        def turns(eng, turn):
            for i in range(-1, 2):
                turn(i, i % 2, i + 1 < PAIRS, 0 <= i < PAIRS, 0 <= i - 1 < PAIRS, 0 <= i - 2 < PAIRS)
            with eng.Fori(1, 3) as k:
                turn(2 * k, 0, True, True, True, True)
                turn(2 * k + 1, 1, True, True, True, True)
            for i in range(6, PAIRS + 2):
                turn(i, i % 2, i + 1 < PAIRS, 0 <= i < PAIRS, 0 <= i - 1 < PAIRS, 0 <= i - 2 < PAIRS)

        def v_window(dy, dx):
            at = (1 + dy) * VP + 1 + dx
            return v_grid[:, at:at + VROWS * VP].rearrange("c (r w) -> c r w", w=VP)[:, :, 0:W]

        block = ctx.enter_context(nc.Block())

        @block.sync
        def _(eng):
            eng.dma_start(x_sb[:, 0, :].rearrange("c (b t) -> c b t", b=2), x_dram[0]).then_inc(in_x[0], 16)
            eng.dma_start(wdw_all[:, :], w_dw[0:QK].rearrange("o a b c -> (o a b c)").unsqueeze(0)
                          .broadcast_to([C, QK * TAPS])).then_inc(in_dw, 16)
            eng.dma_start(x_sb[:, 1, :].rearrange("c (b t) -> c b t", b=2), x_dram[1]).then_inc(in_x[1], 16)
            for i in range(2, PAIRS):
                eng.wait_ge(in_x[i % 2], x_landed(i - 2, i % 2))
                eng.dma_start(x_sb[:, i, :].rearrange("c (b t) -> c b t", b=2), x_dram[i])\
                   .then_inc(in_x[i % 2], 16)
            with eng.Fori(0, PAIRS // 2) as k:
                for p in range(2):
                    i = 2 * k + p
                    eng.wait_ge(y_taken, i + 1)
                    eng.dma_start(out_dram[i], out_sb[p][:, :].rearrange("c (b t) -> c b t", b=2))\
                       .then_inc(stored[p], 16)
            for p in range(2):
                eng.wait_ge(stored[p], 16 * PAIRS // 2)

        @block.scalar
        def _(eng):
            eng.dma_start(wqkv_sb[:, :, :], w_qkv.rearrange("(s o) c -> o s c", s=3)).then_inc(in_w, 16)
            eng.dma_start(wdw_sb[:, :, :], w_dw.rearrange("(s o) a b c -> o s (a b c)", s=3)).then_inc(in_w, 16)
            eng.dma_start(cst[:, :], consts).then_inc(in_w, 16)

            eng.sem_inc(hid_free, 2)

            for g in range(3):
                eng.wait_ge(wc_full, g + 1)
                eng.copy(wc_hi[:, 3 * g:3 * g + 3, :], wc[:, 3 * g:3 * g + 3, :]).then_inc(wc_hi_set, 1)
                if g == 0:
                    eng.copy(wv_hi[:, :], sc_ps[0:C, QK:3 * C]).then_inc(wv_set, 1)

            def copy_late():
                eng.wait_ge(late_T, 1)
                eng.copy(wprojT[:, :], out_ps[0:C, 0:C])
                eng.copy(w1T[:, :, :], hid_ps[0][0:C, 0:ED].rearrange("p (m d) -> p m d", m=MT))
                eng.copy(w2T[:, :, :], hid_ps[1][:, 0:MT * C].rearrange("p (m d) -> p m d", m=MT))\
                   .then_inc(late_set, 1)

            def turn(i, par, nxt, conv, att, moe):
                q = 1 - par
                eng.wait_ge(mean_ready, i + 2)
                eng.activation(dev2[:, :], small_ps[0:C, DEVI:DEVI + 4], ACT.Square).then_inc(dev_ready, 1)
                if conv:
                    wait(eng, tap_done, 8 * i)
                    eng.wait_ge(v_ready, i + 1)
                    if isinstance(i, int) and i == 0:
                        eng.wait_ge(pads_set, 2)
                    grid = v_grid[:, VP:VP + 2 * (H + 1) * VP].rearrange(
                        "c (b h w) -> c b h w", b=2, w=VP)[:, :, 0:H, 1:W + 1]
                    eng.copy(grid, v_ps[0:C, :].rearrange("c (b h w) -> c b h w", b=2, w=W))\
                       .then_inc(v_taken, 1)
                    eng.wait_ge(v_taken, i + 1)
                    wait(eng, out_done, i - 1)
                    eng.activation(v_acc[par][:, :, :], v_window(0, 0), ACT.Copy,
                                   scale=v_taps[:, 4:5]).then_inc(v_init, 1)
                if att:
                    eng.wait_ge(sc_ready, i)
                    eng.activation(sc_exp[:, :, :], sc_in[:, :, :], ACT.Exp).then_inc(exp_ready, 1)
                if conv:
                    take_qk(i, 0)
                if att:
                    eng.wait_ge(mix_done, i)
                    wait(eng, out_done, i - 1)
                    eng.copy(mix_sb[:, :, :], small_ps[0:C, MIX:MIX + QK].rearrange("p (b o) -> p b o", b=2))\
                       .then_inc(mix_ready, 1)
                if nxt:
                    eng.wait_ge(xs_ready, i + 2)
                    wait(eng, tile_done, 4 * i)
                    if isinstance(i, int) and i <= 0:
                        eng.wait_ge(pads_set, 2)
                    src = xs[q][:, :].rearrange("c (b h w) -> c b h w", b=2, w=W)
                    eng.copy(inner(x_hi[q], 1), src).then_inc(hi_mid, 1)
                    eng.copy(inner(x_hi[q], 0)[:, :, :, 1:W], src[:, :, :, 0:W - 1])
                    eng.copy(inner(x_hi[q], 2)[:, :, :, 0:W - 1], src[:, :, :, 1:W]).then_inc(hi_ready, 1)
                if conv:
                    take_qk(i, 1)
                if isinstance(i, int) and i == -1:
                    copy_late()
                if moe:
                    for m in range(MT):
                        eng.wait_ge(hid_done, MT * (i - 2) + m + 1)
                        eng.activation(hidden[:, i - 2, m, :], hid_ps[(par + m) % 2][:, :], ACT.Relu,
                                       bias=b1_sb[:, m:m + 1], scale=1.0 / X_SCALE).then_inc(hid_free, 1)

            def take_qk(i, b):
                eng.wait_ge(tile_done, TILES * i + 2 * b + 2)
                wait(eng, gram_done, i)
                src = qk_ps[b][:, 0:2 * QK].rearrange("p (t o) -> p t o", t=2)
                eng.copy(qk_sb[:, 2 * b:2 * b + 2, :], src)
                eng.activation(qk_sq[:, 2 * b:2 * b + 2, :], src, ACT.Square).then_inc(qk_taken, 1)

            turns(eng, turn)

            eng.wait_ge(g_step, 2)
            eng.activation(g_exp[:, :, :], g_in[:, :, :], ACT.Exp).then_inc(g_exp_ready, 1)
            eng.wait_ge(g_step, TOP_DIFF)
            eng.activation(top_exp[:, :], top_diff[:, :], ACT.Exp).then_inc(top_exp_ready, 1)
            for n in range(4):
                eng.wait_ge(uT_done, n + 1)
                eng.copy(u_sb[:, n * 1024:(n + 1) * 1024],
                         bank[n][0:U, :].bitcast(BF16)[:, 0:1024]).then_inc(u_taken, 1)

        @block.gpsimd
        def _(eng):
            eng.memset(ones[:, :], 1.0)
            eng.memset(minus_half[:, :], -0.5)
            eng.memset(mv[:, :, :], 1.0).then_inc(ones_set, 1)
            for p in range(2):
                eng.memset(x_hi[p][:, :, :, :, :], 0.0)
                eng.memset(x_lo[p][:, :, :, :, :], 0.0)
            eng.memset(v_grid[:, :], 0.0).then_inc(pads_set, 2)
            for dst, src in ((wproj_sb[:, :], w_proj), (gate_w_sb[:, :], gate_w),
                             (w1_sb[:, :, :], w1.rearrange("e d c -> (e d) c").rearrange("(m p) c -> p m c", p=128)),
                             (w2_sb[:, :].rearrange("p (e d) -> p e d", e=EXPERTS), w2.rearrange("e o d -> o e d")),
                             (b2_sb[:, :], b2),
                             (gate_b_sb[:, :], gate_b.unsqueeze(0).broadcast_to([128, EXPERTS]))):
                eng.dma_start(dst, src).then_inc(in_late, 16)
            eng.dma_start(b1_sb[:, :], b1.rearrange("e d -> (e d)").rearrange("(m p) -> p m", p=128),
                          allow_slow_non_contiguous=True).then_inc(in_late, 16)
            for h in range(HEADS):
                eng.dma_start(temp_sb[D * h:D * h + D, :],
                              temperature[0, h:h + 1].rearrange("h a b -> h (a b)").broadcast_to([D, 1]))\
                   .then_inc(in_late, 16)

            def turn(i, par, nxt, conv, att, moe):
                q = 1 - par
                if att:
                    eng.wait_ge(norm2_ready, i)
                    eng.tensor_tensor(rnorm[:, :], norm2[:, :], minus_half[:, :], ALU.pow).then_inc(rnorm_ready, 1)
                eng.wait_ge(eps_ready, i + 2)
                eng.tensor_tensor(rstd[:, :], var_eps[:, :], minus_half[:, 0:4], ALU.pow).then_inc(rstd_ready, 1)
                if nxt:
                    wait_apart(eng, lo_mid, i + 2)
                    src = inner(x_lo[q], 1)
                    eng.tensor_copy(inner(x_lo[q], 0)[:, :, :, 1:W], src[:, :, :, 0:W - 1])
                    eng.tensor_copy(inner(x_lo[q], 2)[:, :, :, 0:W - 1], src[:, :, :, 1:W]).then_inc(lo_ready, 1)

            turns(eng, turn)

        @block.tensor
        def _(eng):
            eng.wait_ge(in_w, 48)
            eng.wait_ge(prep, 5)
            for s in range(3):
                mm = eng.transpose(sc_ps[0:C, s * C:(s + 1) * C], wqkv_scaled[:, s, :], const("ident", C)[:, 0:C])
            mm.then_inc(wT_ready, 1)

            def prepare_late():
                eng.wait_ge(prep, 7)
                eng.wait_ge(wc_full, 3)
                eng.wait_ge(wv_set, 2)
                eng.matmul(sc_ps[0:C, 3 * C:3 * C + D], const("head", C), k_floor_diag[:, :],
                           start=True, stop=True).then_inc(kfl_ready, 1)
                eng.wait_ge(in_late, 16 * 15)
                eng.transpose(out_ps[0:C, 0:C], wproj_sb[:, :], const("ident", C)[:, 0:C])
                for m in range(MT):
                    eng.transpose(hid_ps[0][0:C, m * 128:(m + 1) * 128], w1_sb[:, m, :], const("ident", 128))
                    mm = eng.transpose(hid_ps[1][:, m * C:(m + 1) * C], w2_sb[:, m * 128:(m + 1) * 128],
                                       const("ident", C)[:, 0:C])
                mm.then_inc(late_T, 1)

            def conv_tile(i, par, n):
                b, half = n // 2, n % 2
                if half == 0:
                    wait(eng, qk_taken, 2 * i + b - 1)
                ps = qk_ps[b][:, half * QK:(half + 1) * QK]
                for t in range(TAPS):
                    dy, dx = t // 3, t % 3
                    r = 8 * half + dy
                    hi = x_hi[par][:, dx, b, r:r + 8, :].rearrange("c h w -> c (h w)")
                    lo = x_lo[par][:, dx, b, r:r + 8, :].rearrange("c h w -> c (h w)")
                    if isinstance(i, int) and i == 0 and n == 0 and t % 3 == 0:
                        eng.wait_ge(wc_hi_set, t // 3 + 1)
                        eng.wait_ge(wc_lo_set, t // 3 + 1)
                    eng.matmul(ps, hi, wc_hi[:, t, :], start=(t == 0), stop=False)
                    eng.matmul(ps, hi, wc_lo[:, t, :], start=False, stop=False)
                    mm = eng.matmul(ps, lo, wc_hi[:, t, :], start=False, stop=(t == TAPS - 1))
                mm.then_inc(tile_done, 1)

            def turn(i, par, nxt, conv, att, moe):
                eng.wait_ge(mv_ready, i + 2)
                wait(eng, norm_done, i + 1)
                wait(eng, logit_free, i - 1)
                eng.matmul(small_ps[0:C, MEAN:MEAN + 4], const("avg", C), mv[:, :, 0], start=True, stop=True)
                eng.matmul(small_ps[0:C, DEVI:DEVI + 4], const("dev", C), mv[:, :, 0], start=True, stop=True)\
                   .then_inc(mean_ready, 1)
                if isinstance(i, int) and i == -1:
                    prepare_late()
                if conv:
                    eng.wait_ge(hi_ready, i + 1)
                    eng.wait_ge(lo_ready, i + 1)
                    wait(eng, v_taken, i)
                    if isinstance(i, int) and i == 0:
                        eng.wait_ge(wv_set, 2)
                    for n, (wt, xt) in enumerate(((wv_hi, x_hi), (wv_lo, x_hi), (wv_hi, x_lo))):
                        mm = eng.matmul(v_ps[0:C, :], wt[:, :],
                                        xt[par][:, 1, :, 1:H + 1, :].rearrange("c b h w -> c b (h w)"),
                                        start=(n == 0), stop=(n == 2))
                    mm.then_inc(v_ready, 1)
                if att:
                    eng.wait_ge(qk_taken, 2 * i)
                    wait(eng, gram_taken, i - 1)
                    if isinstance(i, int) and i == 1:
                        eng.wait_ge(kfl_set, 1)
                    for b in range(2):
                        for kind in range(3):
                            for h in range(2):
                                t = 2 * b + h
                                if kind == 0:
                                    o, l, r = sc_ps[0:C, b * C:(b + 1) * C], qk_sb[:, t, 0:C], qk_sb[:, t, C:QK]
                                elif kind == 1:
                                    o, l, r = sc_ps[0:C, (2 + b) * C:(3 + b) * C], ones[:, 0:C], qk_sq[:, t, C:QK]
                                else:
                                    o, l, r = sc_ps[0:C, 4 * C + b:4 * C + b + 1], qk_sq[:, t, 0:C], ones[:, 0:1]
                                mm = eng.matmul(o, l, r, start=(h == 0), stop=(h == 1))
                    mm.then_inc(gram_done, 1)
                if conv:
                    conv_tile(i, par, 0)
                eng.wait_ge(vd_ready, i + 2)
                eng.matmul(small_ps[0:C, VAR:VAR + 4], const("avg", C), var_dev[:, :], start=True, stop=True)\
                   .then_inc(var_ready, 1)
                if conv:
                    conv_tile(i, par, 1)
                if att:
                    eng.wait_ge(attn_ready, i)
                    eng.wait_ge(norm_done, i + 2)
                    if isinstance(i, int) and i == 1:
                        eng.wait_ge(late_set, 1)
                    for b in range(2):
                        mm = eng.matmul(small_ps[0:C, MIX + b * C:MIX + (b + 1) * C], attn[:, b, :], wprojT[:, :],
                                        start=True, stop=True)
                    mm.then_inc(mix_done, 1)
                if conv:
                    conv_tile(i, par, 2)
                if att:
                    eng.wait_ge(mix_ready, i)
                    eng.wait_ge(tap_done, 8 * i)
                    wait(eng, x1_done, i - 1)
                    for b in range(2):
                        mm = eng.matmul(out_ps[0:C, b * HW:(b + 1) * HW], mix_sb[:, b, :],
                                        v_acc[1 - par][:, b * (H + 1):b * (H + 1) + H, :].rearrange("c h w -> c (h w)"),
                                        start=True, stop=True)
                    mm.then_inc(out_done, 1)
                if conv:
                    conv_tile(i, par, 3)
                if moe:
                    eng.wait_ge(xn2_ready, i - 1)
                    wait(eng, mix_ready, i if att else PAIRS)
                    if not att:
                        eng.wait_ge(norm_done, i + 2)
                    for t in range(TILES):
                        mm = eng.matmul(small_ps[:, LOGIT + 4 * t:LOGIT + 4 * t + 4], xn2[:, t * 128:(t + 1) * 128],
                                        gate_w_sb[:, :], start=True, stop=True)
                    mm.then_inc(gate_done, 1)
                    for m in range(MT):
                        eng.wait_ge(hid_free, MT * (i - 2) + m + 1)
                        if isinstance(i, int) and i == 2 and m == 0:
                            eng.wait_ge(late_set, 1)
                        eng.matmul(hid_ps[(par + m) % 2][:, :], w1T[:, m, :], xn2[:, :], start=True, stop=True)\
                           .then_inc(hid_done, 1)

            turns(eng, turn)

            eng.wait_ge(present_ready, 1)
            eng.wait_ge(logit_free, PAIRS + 1)
            eng.matmul(small_ps[0:U, 0:2 * EXPERTS], ones[:, 0:U], present[:, :, :].rearrange("p r e -> p (r e)"),
                       start=True, stop=True)
            for r in range(2):
                mm = eng.matmul(small_ps[0:EXPERTS, 16 + r * URANK:16 + (r + 1) * URANK], present[:, r, :],
                                ones[:, 0:URANK], start=True, stop=True)
            mm.then_inc(count_done, 1)
            eng.wait_ge(on_cols_ready, 1)
            eng.wait_ge(x1_done, PAIRS)
            eng.matmul(out_ps[0:U, 0:C], on_cols[:, :], b2_sb[:, :], start=True, stop=True).then_inc(bias_done, 1)
            eng.wait_ge(u_ready, 1)
            eng.wait_ge(gram_taken, PAIRS)
            eng.wait_ge(qk_taken, 2 * PAIRS)
            eng.wait_ge(v_taken, PAIRS)
            for n in range(4):
                for s in range(8):
                    mm = eng.transpose(bank[n][0:U, :].bitcast(BF16)[:, s * 128:(s + 1) * 128],
                                       u_tok[:, 8 * n + s, :], ident_bf[:, :])
                mm.then_inc(uT_done, 1)

            def coefs(i):
                for m in range(MT):
                    wait_apart(eng, mixed_done, MT * i + m - MT + 1)
                    eng.matmul(bank[m][:, :], spread[:, m * 128:(m + 1) * 128], u_sb[:, bass.ts(i, T)],
                               start=True, stop=True).then_inc(coef_done, 1)

            def second(i, par):
                wait_apart(eng, y_taken, i - 1)
                ps = hid_ps[par][0:C, :]
                eng.matmul(ps, bias_u[:, :], u_sb[:, bass.ts(i, T)], start=True, stop=False)
                for m in range(MT):
                    eng.wait_ge(mixed_done, MT * i + m + 1)
                    mm = eng.matmul(ps, w2T[:, m, :], h_mixed[par][:, m, :], start=False, stop=(m == MT - 1))
                mm.then_inc(y_done, 1)

            eng.wait_ge(spread_ready, 1)
            eng.wait_ge(u_taken, 4)
            coefs(0)
            eng.wait_ge(bias_ready, 1)
            eng.wait_ge(hid_free, MT * PAIRS + 2)
            coefs(1)
            second(0, 0)
            coefs(2)
            second(1, 1)
            with eng.Fori(1, PAIRS // 2 - 1) as k:
                coefs(2 * k + 1)
                second(2 * k, 0)
                coefs(2 * k + 2)
                second(2 * k + 1, 1)
            coefs(PAIRS - 1)
            second(PAIRS - 2, 0)
            second(PAIRS - 1, 1)

        @block.vector
        def _(eng):
            eng.sem_inc(logit_free, 1)

            eng.wait_ge(in_w, 48)
            eng.tensor_reduce(max_w[:, :], wqkv_sb[:, :, :], AX.X, ALU.max, apply_absolute_value=True)
            eng.tensor_reduce(max_dw[:, :], wdw_sb[:, :, :], AX.X, ALU.max, apply_absolute_value=True)\
               .then_inc(prep, 1)
            eng.wait_ge(prep, 1)
            eng.tensor_tensor(row_max[:, 0:2], max_w[:, 0:2], max_dw[:, 0:2], ALU.mult)
            eng.tensor_copy(row_max[:, 2:3], max_w[:, 2:3]).then_inc(prep, 1)
            eng.wait_ge(prep, 2)
            eng.tensor_scalar(row_max[:, :], row_max[:, :], TINY, 1.0 / W_SCALE, ALU.max, ALU.mult).then_inc(prep, 1)
            eng.wait_ge(prep, 3)
            eng.reciprocal(row_scale[:, :], row_max[:, :]).then_inc(prep, 1)
            eng.wait_ge(prep, 4)
            eng.tensor_tensor(wqkv_scaled[:, :, :], wqkv_sb[:, :, :],
                              row_scale[:, :].unsqueeze(2).broadcast_to([C, 3, C]), ALU.mult).then_inc(prep, 1)
            eng.tensor_scalar(v_taps[:, :], wdw_sb[:, 2, :], row_max[:, 2:3], 1.0 / X_SCALE, ALU.mult, ALU.mult)
            eng.tensor_scalar(floors[:, :], row_scale[:, 0:2], L2_EPS * X_SCALE, None, ALU.mult).then_inc(prep, 1)
            eng.wait_ge(prep, 6)
            eng.tensor_tensor(floors[:, :], floors[:, :], floors[:, :], ALU.mult).then_inc(floors_set, 1)
            eng.wait_ge(floors_set, 1)
            eng.tensor_scalar(k_floor_diag[:, :], const("slot", C), floors[:, 1:2], None, ALU.mult).then_inc(prep, 1)
            eng.wait_ge(wT_ready, 1)
            eng.wait_ge(in_dw, 16)
            for g in range(3):
                taps = wdw_all[:, :].rearrange("p (o t) -> p t o", t=TAPS)[:, 3 * g:3 * g + 3, :]
                eng.tensor_tensor(wc[:, 3 * g:3 * g + 3, :], taps,
                                  sc_ps[0:C, 0:QK].unsqueeze(1).broadcast_to([C, 3, QK]), ALU.mult)\
                   .then_inc(wc_full, 1)
                eng.wait_ge(wc_hi_set, g + 1)
                eng.tensor_tensor(wc_lo[:, 3 * g:3 * g + 3, :], wc[:, 3 * g:3 * g + 3, :],
                                  wc_hi[:, 3 * g:3 * g + 3, :], ALU.subtract).then_inc(wc_lo_set, 1)
                if g == 0:
                    eng.wait_ge(wv_set, 1)
                    eng.tensor_tensor(wv_lo[:, :], sc_ps[0:C, QK:3 * C], wv_hi[:, :], ALU.subtract)\
                       .then_inc(wv_set, 1)

            def turn(i, par, nxt, conv, att, moe):
                q = 1 - par
                a, m = i - 1, i - 2
                if nxt:
                    wait_apart(eng, in_x[q], x_landed(i + 1, q))
                    for b in range(2):
                        s = eng.bn_stats(stats[:, b, :], x_sb[:, i + 1, b * HW:(b + 1) * HW])
                if moe:
                    wait_apart(eng, x1_done, i - 1)
                    for b in range(2):
                        s = eng.bn_stats(stats[:, 2 + b, :], x_sb[:, m, b * HW:(b + 1) * HW])
                if nxt or moe:
                    s.then_inc(stats_done, 1)
                else:
                    eng.sem_inc(stats_done, 1)
                wait_apart(eng, stats_done, i + 2)
                if isinstance(i, int) and i == -1:
                    eng.wait_ge(ones_set, 1)
                for b in ((0, 1) if nxt else ()) + ((2, 3) if moe else ()):
                    s = eng.bn_aggr(mv[:, b, :], stats[:, b, :])
                if nxt or moe:
                    s.then_inc(mv_ready, 1)
                else:
                    eng.sem_inc(mv_ready, 1)
                eng.wait_ge(mv_ready, i + 2)
                eng.wait_ge(dev_ready, i + 2)
                eng.tensor_tensor(var_dev[:, :], mv[:, :, 1], dev2[:, :], ALU.add).then_inc(vd_ready, 1)
                if att:
                    eng.wait_ge(gram_done, i)
                    if isinstance(i, int) and i == 1:
                        eng.wait_ge(kfl_ready, 1)
                    eng.tensor_tensor(masked[:, :, :], sc_ps[0:C, 0:4 * C].rearrange("p (s e) -> p s e", s=4),
                                      const("head", C).unsqueeze(1).broadcast_to([C, 4, C]), ALU.mult)
                    eng.tensor_scalar(norm2[:, 2 * D:2 * D + 2], sc_ps[0:C, 4 * C:4 * C + 2], floors[:, 0:1], None,
                                      ALU.max).then_inc(gram_taken, 1)
                    eng.wait_ge(gram_taken, i)
                    eng.tensor_reduce(picked[:, :, :], masked[:, :, :].rearrange("p s (h e) -> p s e h", h=HEADS),
                                      AX.X, ALU.add).then_inc(sm_step, 1)
                    eng.wait_ge(sm_step, SM * a + 1)
                    eng.tensor_tensor(norm2[:, 0:2 * D].rearrange("p (b e) -> p b e", b=2), picked[:, 2:4, :],
                                      k_floor[:, :].unsqueeze(1).broadcast_to([C, 2, D]), ALU.max)\
                       .then_inc(norm2_ready, 1)
                    eng.wait_ge(rnorm_ready, i)
                    eng.tensor_scalar(q_fac[:, :], rnorm[:, 2 * D:2 * D + 2], temp_sb[:, 0:1], None, ALU.mult)
                    eng.tensor_tensor(sc_k[:, :, :], picked[:, 0:2, :],
                                      rnorm[:, 0:2 * D].rearrange("p (b e) -> p b e", b=2), ALU.mult)\
                       .then_inc(sm_step, 1)
                    eng.wait_ge(sm_step, SM * a + 2)
                    eng.tensor_tensor(sc_qk[:, :, :], sc_k[:, :, :], q_fac[:, :].unsqueeze(2).broadcast_to([C, 2, D]),
                                      ALU.mult).then_inc(sm_step, 1)
                    eng.wait_ge(sm_step, SM * a + 3)
                    eng.tensor_reduce(sc_max[:, :], sc_qk[:, :, :], AX.X, ALU.max).then_inc(sm_step, 1)
                    eng.wait_ge(sm_step, SM * a + 4)
                    eng.tensor_tensor(sc_in[:, :, :], sc_qk[:, :, :], sc_max[:, :].unsqueeze(2).broadcast_to([C, 2, D]),
                                      ALU.subtract).then_inc(sc_ready, 1)
                if conv:
                    taps(i, par, 0, 2)
                if att:
                    eng.wait_ge(exp_ready, i)
                    eng.tensor_reduce(sc_sum[:, :], sc_exp[:, :, :], AX.X, ALU.add).then_inc(sm_step, 1)
                    eng.wait_ge(sm_step, SM * a + 5)
                    eng.reciprocal(sc_rec[:, :], sc_sum[:, :]).then_inc(sm_step, 1)
                    eng.wait_ge(sm_step, SM * a + 6)
                    eng.tensor_tensor(probs[:, :, :], sc_exp[:, :, :], sc_rec[:, :].unsqueeze(2).broadcast_to([C, 2, D]),
                                      ALU.mult).then_inc(sm_step, 1)
                    eng.wait_ge(sm_step, SM * a + 7)
                    wait(eng, mix_done, i - 1)
                    for b in range(2):
                        s = eng.tensor_tensor(attn[:, b, :].rearrange("p (h e) -> p h e", h=HEADS),
                                              probs[:, b, :].unsqueeze(1).broadcast_to([C, HEADS, D]),
                                              const("head", C).rearrange("p (h e) -> p h e", h=HEADS), ALU.mult)
                    s.then_inc(attn_ready, 1)
                eng.wait_ge(var_ready, i + 2)
                eng.tensor_scalar(var_eps[:, :], small_ps[0:C, VAR:VAR + 4], GN_EPS, X_SCALE ** -2, ALU.add, ALU.mult)\
                   .then_inc(eps_ready, 1)
                if conv:
                    taps(i, par, 2, 3)
                eng.wait_ge(rstd_ready, i + 2)
                eng.scalar_tensor_tensor(out=shift[:, :], in0=small_ps[0:C, MEAN:MEAN + 4], scalar=-1.0,
                                         in1=rstd[:, :], op0=ALU.mult, op1=ALU.mult).then_inc(norm_done, 1)
                eng.wait_ge(norm_done, i + 2)
                if nxt:
                    wait(eng, hi_ready, i)
                    for b in range(2):
                        s = eng.tensor_scalar(xs[q][:, b * HW:(b + 1) * HW], x_sb[:, i + 1, b * HW:(b + 1) * HW],
                                              rstd[:, b:b + 1], shift[:, b:b + 1], ALU.mult, ALU.add)
                    s.then_inc(xs_ready, 1)
                if moe:
                    eng.wait_ge(hid_free, MT * m + 2)
                    for b in range(2):
                        s = eng.tensor_scalar(xn2[:, b * HW:(b + 1) * HW], x_sb[:, m, b * HW:(b + 1) * HW],
                                              rstd[:, 2 + b:3 + b], shift[:, 2 + b:3 + b], ALU.mult, ALU.add)
                    s.then_inc(xn2_ready, 1)
                if conv:
                    taps(i, par, 3, 5)
                if nxt:
                    if isinstance(i, int) and i <= 0:
                        eng.wait_ge(pads_set, 2)
                    eng.wait_ge(hi_mid, i + 2)
                    wait(eng, tile_done, 4 * i)
                    eng.tensor_tensor(inner(x_lo[q], 1), xs[q][:, :].rearrange("c (b h w) -> c b h w", b=2, w=W),
                                      inner(x_hi[q], 1), ALU.subtract).then_inc(lo_mid, 1)
                if conv:
                    taps(i, par, 5, 8)
                if att:
                    eng.wait_ge(out_done, i)
                    eng.tensor_tensor(x_sb[:, a, :], x_sb[:, a, :], out_ps[0:C, :], ALU.add).then_inc(x1_done, 1)
                if isinstance(i, int) and i == -1:
                    eng.wait_ge(kfl_ready, 1)
                    eng.tensor_copy(k_floor[:, :], sc_ps[0:C, 3 * C:3 * C + D]).then_inc(kfl_set, 1)
                    eng.wait_ge(kfl_set, 1)
                if moe:
                    eng.wait_ge(gate_done, i - 1)
                    eng.scalar_tensor_tensor(
                        out=logits[:, m, :, :],
                        in0=small_ps[:, LOGIT:LOGIT + 4 * TILES].rearrange("p (t e) -> p t e", t=TILES),
                        scalar=1.0 / X_SCALE, in1=gate_b_sb[:, :].unsqueeze(1).broadcast_to([128, TILES, EXPERTS]),
                        op0=ALU.mult, op1=ALU.add).then_inc(logit_free, 1)

            SM = 7
            OUTER = [(dy, dx) for dy in (-1, 0, 1) for dx in (-1, 0, 1) if (dy, dx) != (0, 0)]

            def taps(i, par, lo, hi):
                if lo == 0:
                    eng.wait_ge(v_init, i + 1)
                for n in range(lo, hi):
                    dy, dx = OUTER[n]
                    t = 3 * (dy + 1) + dx + 1
                    wait(eng, tap_done, 8 * i + n)
                    eng.scalar_tensor_tensor(out=v_acc[par][:, :, :], in0=v_window(dy, dx), scalar=v_taps[:, t:t + 1],
                                             in1=v_acc[par][:, :, :], op0=ALU.mult, op1=ALU.add).then_inc(tap_done, 1)

            turns(eng, turn)

            steps = [0]

            def step(ins):
                steps[0] += 1
                ins.then_inc(g_step, 1)
                eng.wait_ge(g_step, steps[0])

            flat = logits[:, :, :, :].rearrange("p i t e -> p (i t) e")
            eng.wait_ge(logit_free, PAIRS + 1)
            step(eng.tensor_reduce(g_max[:, :], flat, AX.X, ALU.max))
            step(eng.tensor_tensor(g_in[:, :, :], flat, g_max[:, :].unsqueeze(2).broadcast_to([128, NT, EXPERTS]),
                                   ALU.subtract))
            eng.wait_ge(g_exp_ready, 1)
            step(eng.tensor_reduce(g_sum[:, :], g_exp[:, :, :], AX.X, ALU.add))
            step(eng.reciprocal(g_rec[:, :], g_sum[:, :]))
            step(eng.tensor_tensor(g_prob[:, :, :], g_exp[:, :, :],
                                   g_rec[:, :].unsqueeze(2).broadcast_to([128, NT, EXPERTS]), ALU.mult))
            every = [128, NT, EXPERTS, EXPERTS]
            score_j = g_prob[:, :, :].unsqueeze(2).broadcast_to(every)
            score_e = g_prob[:, :, :].unsqueeze(3).broadcast_to(every)
            step(eng.tensor_tensor(beats[:, :, :, :], score_j, score_e, ALU.is_gt))
            step(eng.tensor_tensor(ties[:, :, :].rearrange("p t (e j) -> p t e j", e=EXPERTS), score_j, score_e,
                                   ALU.is_equal))
            step(eng.tensor_tensor(beaten[:, :, :], ties[:, :, :],
                                   const("tri", 128).unsqueeze(1).broadcast_to([128, NT, 16]), ALU.mult))
            step(eng.tensor_tensor(beaten[:, :, :], beaten[:, :, :],
                                   beats[:, :, :, :].rearrange("p t e j -> p t (e j)"), ALU.add))
            step(eng.tensor_reduce(rank[:, :, :], beaten[:, :, :].rearrange("p t (e j) -> p t e j", e=EXPERTS),
                                   AX.X, ALU.add))
            eng.tensor_scalar(chosen[:, 0, :, :], rank[:, :, :], 0.0, None, ALU.is_equal)
            step(eng.tensor_scalar(chosen[:, 1, :, :], rank[:, :, :], 1.0, None, ALU.is_equal))
            eng.tensor_reduce(present[:, :, :], chosen[:, :, :, :].rearrange("p r t e -> p r e t"), AX.X, ALU.max)\
               .then_inc(present_ready, 1)
            step(eng.tensor_tensor(top_all[:, :, :, :].rearrange("p r t e -> p r (t e)"),
                                   chosen[:, :, :, :].rearrange("p r t e -> p r (t e)"),
                                   g_prob[:, :, :].rearrange("p t e -> p (t e)").unsqueeze(1)
                                   .broadcast_to([128, 2, NT * EXPERTS]), ALU.mult))
            step(eng.tensor_reduce(top[:, :, :], top_all[:, :, :, :], AX.X, ALU.add))
            step(eng.tensor_tensor(top_diff[:, :], top[:, 1, :], top[:, 0, :], ALU.subtract))
            assert steps[0] == TOP_DIFF
            eng.wait_ge(top_exp_ready, 1)
            step(eng.tensor_scalar(top_den[:, :], top_exp[:, :], 1.0, None, ALU.add))
            step(eng.reciprocal(top_w[:, 0, :], top_den[:, :]))
            step(eng.tensor_tensor(top_w[:, 1, :], top_exp[:, :], top_w[:, 0, :], ALU.mult))
            eng.tensor_copy(ident_bf[:, :], const("ident", 128))
            step(eng.tensor_copy(tw_hi[:, :, :], top_w[:, :, :]))
            step(eng.tensor_tensor(tw_rest[:, :, :], top_w[:, :, :], tw_hi[:, :, :], ALU.subtract))
            step(eng.tensor_copy(tw_mid[:, :, :], tw_rest[:, :, :]))
            step(eng.tensor_tensor(tw_lo[:, :, :], tw_rest[:, :, :], tw_mid[:, :, :], ALU.subtract))
            for part, at, n in ((tw_hi, 0, 3), (tw_mid, 3, 2), (tw_lo, 5, 1)):
                s = eng.tensor_copy(
                    u_tok[:, :, :].rearrange("p t (r u) -> p r t u", r=2)[:, :, :, at:at + n],
                    part[:, :, :].unsqueeze(3).broadcast_to([128, 2, NT, n]))
            s.then_inc(u_ready, 1)
            eng.wait_ge(count_done, 1)
            eng.tensor_scalar(on_cols[:, :], small_ps[0:EXPERTS, 16:16 + U], 1.0, None, ALU.min)\
               .then_inc(on_cols_ready, 1)
            step(eng.tensor_scalar(on_rows[:, :], small_ps[0:U, 0:2 * EXPERTS], 1.0, None, ALU.min))
            step(eng.tensor_scalar(spread0[:, :, :], on_rows[:, 0:EXPERTS].unsqueeze(2).broadcast_to([U, EXPERTS, C]),
                                   const("sel", U)[:, 0:1], None, ALU.mult))
            eng.scalar_tensor_tensor(out=spread[:, :].rearrange("p (e d) -> p e d", e=EXPERTS),
                                     in0=on_rows[:, EXPERTS:2 * EXPERTS].unsqueeze(2).broadcast_to([U, EXPERTS, C]),
                                     scalar=const("sel", U)[:, 1:2], in1=spread0[:, :, :],
                                     op0=ALU.mult, op1=ALU.add).then_inc(spread_ready, 1)
            eng.wait_ge(bias_done, 1)
            step(eng.tensor_copy(bias_hi[:, :], out_ps[0:U, 0:C]))
            step(eng.tensor_tensor(bias_rest[:, :], out_ps[0:U, 0:C], bias_hi[:, :], ALU.subtract))
            step(eng.tensor_copy(bias_mid[:, :], bias_rest[:, :]))
            step(eng.tensor_tensor(bias_lo[:, :], bias_rest[:, :], bias_mid[:, :], ALU.subtract))
            step(eng.tensor_scalar(bias_a[:, :], bias_hi[:, :], const("part", U)[:, 0:1], None, ALU.mult))
            step(eng.scalar_tensor_tensor(out=bias_b[:, :], in0=bias_mid[:, :], scalar=const("part", U)[:, 1:2],
                                          in1=bias_a[:, :], op0=ALU.mult, op1=ALU.add))
            eng.scalar_tensor_tensor(out=bias_u[:, :], in0=bias_lo[:, :], scalar=const("part", U)[:, 2:3],
                                     in1=bias_b[:, :], op0=ALU.mult, op1=ALU.add).then_inc(bias_ready, 1)

            eng.wait_ge(hid_free, MT * PAIRS + 2)

            def mix(i, par):
                wait(eng, y_done, i - 1)
                for m in range(MT):
                    eng.wait_ge(coef_done, MT * i + m + 1)
                    eng.tensor_tensor(h_mixed[par][:, m, :], hidden[:, i, m, :], bank[m][:, :], ALU.mult)\
                       .then_inc(mixed_done, 1)

            def add(i, par):
                eng.wait_ge(y_done, i + 1)
                wait(eng, stored[par], 8 * (i - par))
                eng.tensor_tensor(out_sb[par][:, :], x_sb[:, i, :], hid_ps[par][0:C, :], ALU.add)\
                   .then_inc(y_taken, 1)

            mix(0, 0)
            mix(1, 1)
            add(0, 0)
            mix(2, 0)
            add(1, 1)
            with eng.Fori(1, PAIRS // 2 - 1) as k:
                mix(2 * k + 1, 1)
                add(2 * k, 0)
                mix(2 * k + 2, 0)
                add(2 * k + 1, 1)
            mix(PAIRS - 1, 1)
            add(PAIRS - 2, 0)
            add(PAIRS - 1, 1)


def constants():
    import numpy as np
    c = np.arange(C)
    t = {n: np.zeros((128, w), np.float32) for n, w in CONSTS}
    t["ident"][:] = np.eye(128)
    same = (c[:, None] // GROUP == c[None, :] // GROUP) / GROUP
    t["avg"][:C] = same
    t["dev"][:C] = np.eye(C) - same
    t["head"][:C] = c[:, None] // D == c[None, :] // D
    t["slot"][:C] = c[:, None] % D == np.arange(D)[None, :]
    e = np.arange(EXPERTS)
    t["tri"][:] = (e[None, :] < e[:, None]).reshape(1, 16)
    bias_part = [0, 1, 2, 0, 1, 0]
    for k in range(U):
        t["sel"][k, k // URANK] = bias_part[k % URANK] == 0
        t["part"][k, bias_part[k % URANK]] = 1.0
    return np.concatenate([t[n] for n, _ in CONSTS], axis=1)


_INS = ["x", "L0_conv_w_qkv", "L0_conv_w_dw", "L0_conv_w_proj", "L0_conv_temperature", "L1_conv_gate_w",
        "L1_conv_gate_b", "L1_conv_w1", "L1_conv_b1", "L1_conv_w2", "L1_conv_b2"]


def kernel(**inputs):
    import numpy as np
    import concourse.bacc as bacc
    from concourse.bass_utils import run_bass_kernel_spmd

    nc = bacc.Bacc("TRN2", target_bir_lowering=False, num_devices=1)
    arrays, args = {}, []
    named = [(n, np.ascontiguousarray(inputs[n])) for n in _INS] + [("consts", constants())]
    for name, a in named:
        arrays[f"in_{name}"] = a
        args.append(nc.dram_tensor(f"in_{name}", a.shape, mybir.dt.from_np(a.dtype), kind="ExternalInput").ap())
    out = nc.dram_tensor("out_0", (B, C, H, W), F32, kind="ExternalOutput").ap()
    build(nc, *args, out)
    r = run_bass_kernel_spmd(nc, [arrays], core_ids=[0])
    return r.results[0]["out_0"]
```

```python
from contextlib import ExitStack

import concourse.bass as bass
from concourse import mybir

ALU = mybir.AluOpType
ACT = mybir.ActivationFunctionType
AX = mybir.AxisListType
F32 = mybir.dt.float32
F16 = mybir.dt.float16
BF16 = mybir.dt.bfloat16

B, C, H, W = 16, 96, 16, 16
HW = H * W
PAIRS = B // 2
T = 2 * HW
TILES = T // 128
TAPS = 9
HEADS = 8
D = C // HEADS
GROUP = C // 32
EXPERTS = 4
ED = EXPERTS * C
MT = ED // 128
QK = 2 * C
GN_EPS = 1e-5
L2_EPS = 1e-12
X_SCALE = 16.0
W_SCALE = 16.0
TINY = 1e-20
TOP_DIFF = 14
URANK = 6
U = 2 * URANK
VP = W + 1
VROWS = 2 * H + 1

CONSTS = [("ident", 128), ("avg", C), ("dev", C), ("head", C), ("slot", D), ("tri", 16),
          ("sel", 2), ("part", 3)]
CONST_AT = {}
_at = 0
for _n, _w in CONSTS:
    CONST_AT[_n] = (_at, _at + _w)
    _at += _w
CONST_W = _at


def build(nc, x, w_qkv, w_dw, w_proj, temperature, gate_w, gate_b, w1, b1, w2, b2, consts, out):
    ctx = ExitStack()
    with ctx:
        def sb(name, shape, dt=F32):
            return ctx.enter_context(nc.sbuf_tensor(name, shape, dt))

        def sem(name):
            return ctx.enter_context(nc.semaphore(name))

        cst = sb("cst", [128, CONST_W])

        def const(name, parts):
            a, b = CONST_AT[name]
            return cst[0:parts, a:b]

        wqkv_sb = sb("wqkv_sb", [C, 3, C])
        wdw_sb = sb("wdw_sb", [C, 3, TAPS])
        wdw_all = sb("wdw_all", [C, QK * TAPS])
        wproj_sb = sb("wproj_sb", [C, C])
        temp_all = sb("temp_all", [C, HEADS])
        temp_own = sb("temp_own", [C, HEADS])
        temp_sb = sb("temp_sb", [C, 1])
        gate_w_sb = sb("gate_w_sb", [C, EXPERTS])
        gate_b_sb = sb("gate_b_sb", [128, EXPERTS])
        w1_sb = sb("w1_sb", [128, MT, C])
        b1_sb = sb("b1_sb", [128, MT])
        w2_sb = sb("w2_sb", [C, ED])
        b2_sb = sb("b2_sb", [EXPERTS, C])
        ones = sb("ones", [128, 128])
        minus_half = sb("minus_half", [C, 4])
        max_w = sb("max_w", [C, 3])
        max_dw = sb("max_dw", [C, 3])
        row_max = sb("row_max", [C, 3])
        row_scale = sb("row_scale", [C, 3])
        wqkv_scaled = sb("wqkv_scaled", [C, 3, C])
        floors = sb("floors", [C, 2, 2])
        v_taps = sb("v_taps", [C, TAPS])
        wc = sb("wc", [C, TAPS, QK])
        wc_hi = sb("wc_hi", [C, TAPS, QK], F16)
        wc_lo = sb("wc_lo", [C, TAPS, QK], F16)
        wv_hi = sb("wv_hi", [C, C], F16)
        wv_lo = sb("wv_lo", [C, C], F16)
        wprojT = sb("wprojT", [C, C])
        w1T = sb("w1T", [C, MT, 128])
        w2T = sb("w2T", [128, MT, C])

        x_sb = sb("x_sb", [C, PAIRS, T])
        stats = sb("stats", [C, 4, 6])
        mv = sb("mv", [C, 4, 2])
        dev2 = sb("dev2", [C, 4])
        var_dev = sb("var_dev", [C, 4])
        var_eps = sb("var_eps", [C, 4])
        rstd = sb("rstd", [C, 4])
        shift = sb("shift", [C, 4])
        xs = [sb(f"xs{p}", [C, T]) for p in range(2)]
        x_hi = [sb(f"x_hi{p}", [C, 3, 2, H + 2, W], F16) for p in range(2)]
        x_lo = [sb(f"x_lo{p}", [C, 3, 2, H + 2, W], F16) for p in range(2)]
        v_grid = sb("v_grid", [C, (VROWS + 2) * VP + 2])
        v_acc = [sb(f"v_acc{p}", [C, VROWS, W]) for p in range(2)]
        qk_sb = sb("qk_sb", [128, TILES, QK])
        qk_sq = sb("qk_sq", [128, TILES, QK])
        masked = sb("masked", [C, 2, C])
        picked = sb("picked", [C, 2, D])
        norm2 = sb("norm2", [C, 4])
        rnorm = sb("rnorm", [C, 4])
        k_diag = sb("k_diag", [C, 2, D])
        q_fac = sb("q_fac", [C, 2])
        sc_k = sb("sc_k", [C, 2, D])
        sc_qk = sb("sc_qk", [C, 2, D])
        sc_max = sb("sc_max", [C, 2])
        sc_in = sb("sc_in", [C, 2, D])
        sc_exp = sb("sc_exp", [C, 2, D])
        sc_sum = sb("sc_sum", [C, 2])
        sc_rec = sb("sc_rec", [C, 2])
        probs = sb("probs", [C, 2, D])
        attn = sb("attn", [C, 2, C])
        mix_sb = sb("mix_sb", [C, 2, C])
        xn2 = [sb(f"xn2_{p}", [C, T]) for p in range(2)]
        hidden = sb("hidden", [128, PAIRS, MT, T])
        logits = sb("logits", [128, PAIRS, TILES, EXPERTS])
        NT = PAIRS * TILES
        g_max = sb("g_max", [128, NT])
        g_in = sb("g_in", [128, NT, EXPERTS])
        g_exp = sb("g_exp", [128, NT, EXPERTS])
        g_sum = sb("g_sum", [128, NT])
        g_rec = sb("g_rec", [128, NT])
        g_prob = sb("g_prob", [128, NT, EXPERTS])
        beats = sb("beats", [128, NT, EXPERTS, EXPERTS])
        ties = sb("ties", [128, NT, 16])
        beaten = sb("beaten", [128, NT, 16])
        rank = sb("rank", [128, NT, EXPERTS])
        chosen = sb("chosen", [128, 2, NT, EXPERTS])
        present = sb("present", [128, 2, EXPERTS])
        top_all = sb("top_all", [128, 2, NT, EXPERTS])
        top = sb("top", [128, 2, NT])
        top_diff = sb("top_diff", [128, NT])
        top_exp = sb("top_exp", [128, NT])
        top_den = sb("top_den", [128, NT])
        top_w = sb("top_w", [128, 2, NT])
        tw_hi = sb("tw_hi", [128, 2, NT], BF16)
        tw_rest = sb("tw_rest", [128, 2, NT])
        tw_mid = sb("tw_mid", [128, 2, NT], BF16)
        tw_lo = sb("tw_lo", [128, 2, NT], BF16)
        u_tok = sb("u_tok", [128, NT, U], BF16)
        ident_bf = sb("ident_bf", [128, 128], BF16)
        u_sb = sb("u_sb", [U, B * HW], BF16)
        on_rows = sb("on_rows", [U, 2 * EXPERTS])
        on_cols = sb("on_cols", [EXPERTS, U])
        spread0 = sb("spread0", [U, EXPERTS, C])
        spread = sb("spread", [U, ED], BF16)
        bias_hi = sb("bias_hi", [U, C], BF16)
        bias_rest = sb("bias_rest", [U, C])
        bias_mid = sb("bias_mid", [U, C], BF16)
        bias_lo = sb("bias_lo", [U, C], BF16)
        bias_a = sb("bias_a", [U, C])
        bias_b = sb("bias_b", [U, C])
        bias_u = sb("bias_u", [U, C], BF16)
        h_mixed = [sb(f"h_mixed{p}", [128, MT, T]) for p in range(2)]
        out_sb = [sb(f"out_sb{p}", [C, T]) for p in range(2)]

        bank = [ctx.enter_context(nc.psum_tensor(f"bank{n}", [128, 512], F32)) for n in range(8)]
        qk_ps = bank[0:2]
        v_ps = bank[2]
        sc_ps = bank[3]
        small_ps = bank[4]
        out_ps = bank[5]
        hid_ps = bank[6:8]
        MEAN, DEVI, VAR, MIX, LOGIT = 0, 4, 8, 16, 16 + QK
        SQ, RK = QK, QK + 4

        in_w = sem("in_w")
        in_dw = sem("in_dw")
        in_late = sem("in_late")
        in_x = [sem(f"in_x{p}") for p in range(2)]
        ones_set = sem("ones_set")
        pads_set = sem("pads_set")
        prep = sem("prep")
        passed = sem("passed")
        wT_ready = sem("wT_ready")
        wc_full = sem("wc_full")
        wc_hi_set = sem("wc_hi_set")
        wc_lo_set = sem("wc_lo_set")
        wv_set = sem("wv_set")
        floors_set = sem("floors_set")
        in_c = sem("in_c")
        temp_ready = sem("temp_ready")
        late_T = sem("late_T")
        late_set = sem("late_set")
        stats_done = sem("stats_done")
        mv_ready = sem("mv_ready")
        mean_ready = sem("mean_ready")
        dev_ready = sem("dev_ready")
        vd_ready = sem("vd_ready")
        var_ready = sem("var_ready")
        eps_ready = sem("eps_ready")
        rstd_ready = sem("rstd_ready")
        norm_done = sem("norm_done")
        xs_ready = sem("xs_ready")
        hi_mid = sem("hi_mid")
        hi_ready = sem("hi_ready")
        lo_mid = sem("lo_mid")
        lo_ready = sem("lo_ready")
        v_ready = sem("v_ready")
        v_taken = sem("v_taken")
        v_init = sem("v_init")
        tap_done = sem("tap_done")
        tile_done = sem("tile_done")
        qk_taken = sem("qk_taken")
        gram_done = sem("gram_done")
        gram_taken = sem("gram_taken")
        norm2_ready = sem("norm2_ready")
        rnorm_ready = sem("rnorm_ready")
        sm_step = sem("sm_step")
        diag_ready = sem("diag_ready")
        rk_done = sem("rk_done")
        rk_taken = sem("rk_taken")
        sc_ready = sem("sc_ready")
        exp_ready = sem("exp_ready")
        attn_ready = sem("attn_ready")
        mix_done = sem("mix_done")
        mix_ready = sem("mix_ready")
        out_done = sem("out_done")
        x1_done = sem("x1_done")
        xn2_ready = sem("xn2_ready")
        gate_done = sem("gate_done")
        logit_free = sem("logit_free")
        hid_done = sem("hid_done")
        hid_free = sem("hid_free")
        g_step = sem("g_step")
        g_exp_ready = sem("g_exp_ready")
        top_exp_ready = sem("top_exp_ready")
        present_ready = sem("present_ready")
        count_done = sem("count_done")
        on_cols_ready = sem("on_cols_ready")
        bias_done = sem("bias_done")
        spread_ready = sem("spread_ready")
        bias_ready = sem("bias_ready")
        u_ready = sem("u_ready")
        uT_done = sem("uT_done")
        u_taken = sem("u_taken")
        coef_done = sem("coef_done")
        mixed_done = sem("mixed_done")
        y_done = sem("y_done")
        y_taken = sem("y_taken")
        stored = [sem(f"stored{p}") for p in range(2)]

        x_dram = x.rearrange("(i b) c h w -> i c b (h w)", b=2)
        out_dram = out.rearrange("(i b) c h w -> i c b (h w)", b=2)

        def wait(eng, s, value):
            if not isinstance(value, int) or value > 0:
                eng.wait_ge(s, value)

        def wait_apart(eng, s, value):
            wait(eng, s, value)
            if not isinstance(value, int):
                eng.sem_inc(passed, 1)

        def x_landed(pair, parity):
            return 8 * (pair - parity) + 16

        def inner(t, dx):
            return t[:, dx, :, 1:H + 1, :]

        def turns(eng, turn):
            def short(i):
                turn(i, i % 2, i + 1 < PAIRS, 0 <= i < PAIRS, 0 <= i - 1 < PAIRS, 0 <= i - 2 < PAIRS,
                     0 <= i - 3 < PAIRS - 1)

            for i in range(-1, 3):
                short(i)
            with eng.Fori(1, 3) as k:
                turn(2 * k + 1, 1, True, True, True, True, True)
                turn(2 * k + 2, 0, True, True, True, True, True)
            for i in range(7, PAIRS + 2):
                short(i)

        def v_window(dy, dx):
            at = (1 + dy) * VP + 1 + dx
            return v_grid[:, at:at + VROWS * VP].rearrange("c (r w) -> c r w", w=VP)[:, :, 0:W]

        block = ctx.enter_context(nc.Block())

        @block.sync
        def _(eng):
            eng.dma_start(x_sb[:, 0, :].rearrange("c (b t) -> c b t", b=2), x_dram[0]).then_inc(in_x[0], 16)
            eng.dma_start(wdw_all[:, :], w_dw[0:QK].rearrange("o a b c -> (o a b c)").unsqueeze(0)
                          .broadcast_to([C, QK * TAPS])).then_inc(in_dw, 16)
            eng.dma_start(x_sb[:, 1, :].rearrange("c (b t) -> c b t", b=2), x_dram[1]).then_inc(in_x[1], 16)
            for i in range(2, PAIRS):
                eng.wait_ge(in_x[i % 2], x_landed(i - 2, i % 2))
                eng.dma_start(x_sb[:, i, :].rearrange("c (b t) -> c b t", b=2), x_dram[i])\
                   .then_inc(in_x[i % 2], 16)
                if i == 3:
                    for dst, src in ((wproj_sb[:, :], w_proj), (gate_w_sb[:, :], gate_w),
                                     (w1_sb[:, :, :], w1.rearrange("e d c -> (e d) c")
                                      .rearrange("(m p) c -> p m c", p=128)),
                                     (w2_sb[:, :].rearrange("p (e d) -> p e d", e=EXPERTS),
                                      w2.rearrange("e o d -> o e d")),
                                     (b2_sb[:, :], b2),
                                     (gate_b_sb[:, :], gate_b.unsqueeze(0).broadcast_to([128, EXPERTS])),
                                     (temp_all[:, :], temperature.rearrange("a h b c -> a (h b c)")
                                      .broadcast_to([C, HEADS]))):
                        eng.dma_start(dst, src).then_inc(in_late, 16)
                    eng.dma_start(b1_sb[:, :], b1.rearrange("e d -> (e d)").rearrange("(m p) -> p m", p=128),
                                  allow_slow_non_contiguous=True).then_inc(in_late, 16)
            with eng.Fori(0, PAIRS // 2) as k:
                for p in range(2):
                    i = 2 * k + p
                    eng.wait_ge(y_taken, i + 1)
                    eng.dma_start(out_dram[i], out_sb[p][:, :].rearrange("c (b t) -> c b t", b=2))\
                       .then_inc(stored[p], 16)
            for p in range(2):
                eng.wait_ge(stored[p], 16 * PAIRS // 2)

        @block.scalar
        def _(eng):
            eng.dma_start(cst[:, :], consts).then_inc(in_c, 16)
            eng.dma_start(wqkv_sb[:, :, :], w_qkv.rearrange("(s o) c -> o s c", s=3)).then_inc(in_w, 16)
            eng.dma_start(wdw_sb[:, :, :], w_dw.rearrange("(s o) a b c -> o s (a b c)", s=3)).then_inc(in_w, 16)
            eng.sem_inc(hid_free, 2)

            def copy_late():
                eng.wait_ge(late_T, 1)
                eng.copy(wprojT[:, :], out_ps[0:C, 0:C])
                eng.copy(w1T[:, :, :], hid_ps[0][0:C, 0:ED].rearrange("p (m d) -> p m d", m=MT))
                eng.copy(w2T[:, :, :], hid_ps[1][:, 0:MT * C].rearrange("p (m d) -> p m d", m=MT))\
                   .then_inc(late_set, 1)

            def take_v(i, par):
                eng.wait_ge(v_ready, i + 1)
                wait(eng, tap_done, 8 * i)
                if isinstance(i, int) and i == 0:
                    eng.wait_ge(pads_set, 1)
                grid = v_grid[:, VP:VP + 2 * (H + 1) * VP].rearrange(
                    "c (b h w) -> c b h w", b=2, w=VP)[:, :, 0:H, 1:W + 1]
                eng.copy(grid, v_ps[0:C, :].rearrange("c (b h w) -> c b h w", b=2, w=W)).then_inc(v_taken, 1)
                eng.wait_ge(v_taken, i + 1)
                wait(eng, out_done, i - 1)
                if isinstance(i, int) and i == 0:
                    eng.wait_ge(prep, 6)
                eng.activation(v_acc[par][:, :, :], v_window(0, 0), ACT.Copy, scale=v_taps[:, 4:5])\
                   .then_inc(v_init, 1)

            def take_qk(i, b):
                eng.wait_ge(tile_done, TILES * i + 2 * b + 2)
                wait(eng, gram_done, i)
                src = qk_ps[b][:, 0:2 * QK].rearrange("p (t o) -> p t o", t=2)
                eng.copy(qk_sb[:, 2 * b:2 * b + 2, :], src)
                eng.activation(qk_sq[:, 2 * b:2 * b + 2, :], src, ACT.Square).then_inc(qk_taken, 1)

            def relu(m, par):
                for n in range(MT):
                    eng.wait_ge(hid_done, MT * m + n + 1)
                    eng.activation(hidden[:, m, n, :], hid_ps[(par + n) % 2][:, :], ACT.Relu,
                                   bias=b1_sb[:, n:n + 1], scale=1.0 / X_SCALE).then_inc(hid_free, 1)

            def turn(i, par, nxt, conv, att, moe, hid):
                q = 1 - par
                if conv:
                    take_v(i, par)
                eng.wait_ge(mean_ready, i + 2)
                eng.activation(dev2[:, :], small_ps[0:C, DEVI:DEVI + 4], ACT.Square).then_inc(dev_ready, 1)
                if att:
                    eng.wait_ge(sc_ready, i)
                    eng.activation(sc_exp[:, :, :], sc_in[:, :, :], ACT.Exp).then_inc(exp_ready, 1)
                if conv:
                    take_qk(i, 0)
                if nxt:
                    eng.wait_ge(norm_done, i + 2)
                    wait(eng, lo_mid, i)
                    for b in range(2):
                        a = eng.activation(xs[q][:, b * HW:(b + 1) * HW], x_sb[:, i + 1, b * HW:(b + 1) * HW],
                                           ACT.Identity, scale=rstd[:, b:b + 1], bias=shift[:, b:b + 1])
                    a.then_inc(xs_ready, 1)
                    eng.wait_ge(xs_ready, i + 2)
                    wait(eng, tile_done, 4 * i)
                    if isinstance(i, int) and i <= 0:
                        eng.wait_ge(pads_set, i + 2)
                    src = xs[q][:, :].rearrange("c (b h w) -> c b h w", b=2, w=W)
                    eng.copy(inner(x_hi[q], 1), src).then_inc(hi_mid, 1)
                    eng.copy(inner(x_hi[q], 0)[:, :, :, 1:W], src[:, :, :, 0:W - 1])
                    eng.copy(inner(x_hi[q], 2)[:, :, :, 0:W - 1], src[:, :, :, 1:W]).then_inc(hi_ready, 1)
                if moe:
                    eng.wait_ge(norm_done, i + 2)
                    wait(eng, hid_free, MT * (i - 4) + MT + 2)
                    for b in range(2):
                        a = eng.activation(xn2[par][:, b * HW:(b + 1) * HW], x_sb[:, i - 2, b * HW:(b + 1) * HW],
                                           ACT.Identity, scale=rstd[:, 2 + b:3 + b], bias=shift[:, 2 + b:3 + b])
                    a.then_inc(xn2_ready, 1)
                if att:
                    eng.wait_ge(mix_done, i)
                    wait(eng, out_done, i - 1)
                    eng.copy(mix_sb[:, :, :], small_ps[0:C, MIX:MIX + QK].rearrange("p (b o) -> p b o", b=2))\
                       .then_inc(mix_ready, 1)
                if isinstance(i, int) and i == -1:
                    for g in range(3):
                        eng.wait_ge(wc_full, g + 1)
                        eng.copy(wc_hi[:, 3 * g:3 * g + 3, :], wc[:, 3 * g:3 * g + 3, :]).then_inc(wc_hi_set, 1)
                        if g == 0:
                            eng.copy(wv_hi[:, :], v_ps[0:C, 0:C]).then_inc(wv_set, 1)
                if conv:
                    take_qk(i, 1)
                if isinstance(i, int) and i == 0:
                    copy_late()
                if hid:
                    relu(i - 3, q)

            turns(eng, turn)

            eng.wait_ge(g_step, 2)
            eng.activation(g_exp[:, :, :], g_in[:, :, :], ACT.Exp).then_inc(g_exp_ready, 1)
            relu(PAIRS - 1, 1)
            eng.wait_ge(g_step, TOP_DIFF)
            eng.activation(top_exp[:, :], top_diff[:, :], ACT.Exp).then_inc(top_exp_ready, 1)
            for n in range(4):
                eng.wait_ge(uT_done, n + 1)
                eng.copy(u_sb[:, n * 1024:(n + 1) * 1024],
                         bank[n][0:U, :].bitcast(BF16)[:, 0:1024]).then_inc(u_taken, 1)

        @block.gpsimd
        def _(eng):
            eng.memset(mv[:, :, :], 1.0)
            eng.memset(minus_half[:, :], -0.5).then_inc(ones_set, 1)
            for p in range(2):
                for t in (x_hi[p], x_lo[p]):
                    for row in (0, H + 1):
                        eng.memset(t[:, :, :, row, :], 0.0)
                    eng.memset(t[:, 0, :, 1:H + 1, 0:1], 0.0)
                    z = eng.memset(t[:, 2, :, 1:H + 1, W - 1:W], 0.0)
                if p == 0:
                    z = eng.memset(v_grid[:, :], 0.0)
                z.then_inc(pads_set, 1)
            eng.memset(ones[:, :], 1.0).then_inc(ones_set, 1)

            def turn(i, par, nxt, conv, att, moe, hid):
                q = 1 - par
                if att:
                    eng.wait_ge(norm2_ready, i)
                    eng.tensor_tensor(rnorm[:, :], norm2[:, :], minus_half[:, :], ALU.pow).then_inc(rnorm_ready, 1)
                eng.wait_ge(eps_ready, i + 2)
                eng.tensor_tensor(rstd[:, :], var_eps[:, :], minus_half[:, :], ALU.pow).then_inc(rstd_ready, 1)
                if nxt:
                    wait_apart(eng, lo_mid, i + 2)
                    src = inner(x_lo[q], 1)
                    eng.tensor_copy(inner(x_lo[q], 0)[:, :, :, 1:W], src[:, :, :, 0:W - 1])
                    eng.tensor_copy(inner(x_lo[q], 2)[:, :, :, 0:W - 1], src[:, :, :, 1:W]).then_inc(lo_ready, 1)

            turns(eng, turn)

        @block.tensor
        def _(eng):
            def prepare_qkv():
                eng.wait_ge(prep, 5)
                for s in range(3):
                    to = sc_ps[0:C, s * C:(s + 1) * C] if s < 2 else v_ps[0:C, 0:C]
                    mm = eng.transpose(to, wqkv_scaled[:, s, :], const("ident", C)[:, 0:C])
                mm.then_inc(wT_ready, 1)

            def prepare_late():
                eng.wait_ge(in_late, 16 * 8)
                eng.transpose(out_ps[0:C, 0:C], wproj_sb[:, :], const("ident", C)[:, 0:C])
                for m in range(MT):
                    eng.transpose(hid_ps[0][0:C, m * 128:(m + 1) * 128], w1_sb[:, m, :], const("ident", 128))
                    mm = eng.transpose(hid_ps[1][:, m * C:(m + 1) * C], w2_sb[:, m * 128:(m + 1) * 128],
                                       const("ident", C)[:, 0:C])
                mm.then_inc(late_T, 1)

            def conv_taps(i, par, n, first, last):
                b, half = n // 2, n % 2
                if half == 0 and first == 0:
                    wait(eng, qk_taken, 2 * i + b - 1)
                ps = qk_ps[b][:, half * QK:(half + 1) * QK]
                for t in range(first, last):
                    dy, dx = t // 3, t % 3
                    r = 8 * half + dy
                    hi = x_hi[par][:, dx, b, r:r + 8, :].rearrange("c h w -> c (h w)")
                    lo = x_lo[par][:, dx, b, r:r + 8, :].rearrange("c h w -> c (h w)")
                    if isinstance(i, int) and i == 0 and n == 0 and t % 3 == 0:
                        eng.wait_ge(wc_hi_set, t // 3 + 1)
                        eng.wait_ge(wc_lo_set, t // 3 + 1)
                    eng.matmul(ps, hi, wc_hi[:, t, :], start=(t == 0), stop=False, skip_group_check=True)
                    eng.matmul(ps, hi, wc_lo[:, t, :], start=False, stop=False, skip_group_check=True)
                    mm = eng.matmul(ps, lo, wc_hi[:, t, :], start=False, stop=(t == TAPS - 1),
                                    skip_group_check=True)
                if last == TAPS:
                    mm.then_inc(tile_done, 1)

            def norm_means(i):
                eng.wait_ge(mv_ready, i + 2)
                wait(eng, norm_done, i + 1)
                wait(eng, logit_free, i - 1)
                if isinstance(i, int) and i == -1:
                    eng.wait_ge(in_c, 16)
                eng.matmul(small_ps[0:C, MEAN:MEAN + 4], const("avg", C), mv[:, :, 0], start=True, stop=True)
                eng.matmul(small_ps[0:C, DEVI:DEVI + 4], const("dev", C), mv[:, :, 0], start=True, stop=True)\
                   .then_inc(mean_ready, 1)

            def norm_vars(i):
                eng.wait_ge(vd_ready, i + 2)
                eng.matmul(small_ps[0:C, VAR:VAR + 4], const("avg", C), var_dev[:, :], start=True, stop=True)\
                   .then_inc(var_ready, 1)

            def project_v(i, par):
                eng.wait_ge(hi_ready, i + 1)
                eng.wait_ge(lo_ready, i + 1)
                wait(eng, v_taken, i)
                if isinstance(i, int) and i == 0:
                    eng.wait_ge(wv_set, 2)
                for n, (wt, xt) in enumerate(((wv_hi, x_hi), (wv_lo, x_hi), (wv_hi, x_lo))):
                    mm = eng.matmul(v_ps[0:C, :], wt[:, :],
                                    xt[par][:, 1, :, 1:H + 1, :].rearrange("c b h w -> c b (h w)"),
                                    start=(n == 0), stop=(n == 2))
                mm.then_inc(v_ready, 1)

            def gram(i):
                eng.wait_ge(qk_taken, 2 * i)
                wait(eng, rk_taken, i - 1)
                if isinstance(i, int) and i == 1:
                    eng.wait_ge(ones_set, 2)
                for b in range(2):
                    for h in range(2):
                        eng.matmul(sc_ps[0:C, b * C:(b + 1) * C], qk_sb[:, 2 * b + h, 0:C],
                                   qk_sb[:, 2 * b + h, C:QK], start=(h == 0), stop=(h == 1))
                for b in range(2):
                    for kind in range(2):
                        at = SQ + 2 * kind + b
                        for h in range(2):
                            mm = eng.matmul(sc_ps[0:C, at:at + 1], qk_sq[:, 2 * b + h, kind * C:(kind + 1) * C],
                                            ones[:, 0:1], start=(h == 0), stop=(h == 1))
                mm.then_inc(gram_done, 1)

            def spread_rk(i):
                eng.wait_ge(diag_ready, i)
                eng.matmul(sc_ps[0:C, RK:RK + 2 * D], const("head", C), k_diag[:, :, :].rearrange("p b e -> p (b e)"),
                           start=True, stop=True).then_inc(rk_done, 1)

            def mix_heads(i):
                eng.wait_ge(attn_ready, i)
                eng.wait_ge(norm_done, i + 2)
                if isinstance(i, int) and i == 1:
                    eng.wait_ge(late_set, 1)
                for b in range(2):
                    mm = eng.matmul(small_ps[0:C, MIX + b * C:MIX + (b + 1) * C], attn[:, b, :], wprojT[:, :],
                                    start=True, stop=True)
                mm.then_inc(mix_done, 1)

            def apply_mix(i, par):
                eng.wait_ge(mix_ready, i)
                eng.wait_ge(tap_done, 8 * i)
                wait(eng, x1_done, i - 1)
                for b in range(2):
                    mm = eng.matmul(out_ps[0:C, b * HW:(b + 1) * HW], mix_sb[:, b, :],
                                    v_acc[1 - par][:, b * (H + 1):b * (H + 1) + H, :].rearrange("c h w -> c (h w)"),
                                    start=True, stop=True)
                mm.then_inc(out_done, 1)

            def gate(i, par, att):
                eng.wait_ge(xn2_ready, i - 1)
                if att:
                    eng.wait_ge(mix_ready, i)
                else:
                    eng.wait_ge(norm_done, i + 2)
                for t in range(TILES):
                    mm = eng.matmul(small_ps[:, LOGIT + 4 * t:LOGIT + 4 * t + 4], xn2[par][:, t * 128:(t + 1) * 128],
                                    gate_w_sb[:, :], start=True, stop=True)
                mm.then_inc(gate_done, 1)

            def first(m, par):
                for n in range(MT):
                    eng.wait_ge(hid_free, MT * m + n + 1)
                    eng.matmul(hid_ps[(par + n) % 2][:, :], w1T[:, n, :], xn2[par][:, :], start=True, stop=True)\
                       .then_inc(hid_done, 1)

            def turn(i, par, nxt, conv, att, moe, hid):
                if conv:
                    project_v(i, par)
                if att:
                    gram(i)
                if conv:
                    conv_taps(i, par, 0, 0, 5)
                norm_means(i)
                if conv:
                    conv_taps(i, par, 0, 5, TAPS)
                    conv_taps(i, par, 1, 0, 3)
                if att:
                    spread_rk(i)
                norm_vars(i)
                if conv:
                    conv_taps(i, par, 1, 3, TAPS)
                    conv_taps(i, par, 2, 0, TAPS)
                if att:
                    mix_heads(i)
                if conv:
                    conv_taps(i, par, 3, 0, TAPS)
                if isinstance(i, int) and i == -1:
                    prepare_qkv()
                if isinstance(i, int) and i == 0:
                    prepare_late()
                if hid and not conv:
                    first(i - 3, 1 - par)
                if att:
                    apply_mix(i, par)
                if moe:
                    gate(i, par, att)
                if hid and conv:
                    first(i - 3, 1 - par)

            turns(eng, turn)

            first(PAIRS - 1, 1)

            eng.wait_ge(present_ready, 1)
            eng.wait_ge(logit_free, PAIRS + 1)
            eng.matmul(small_ps[0:U, 0:2 * EXPERTS], ones[:, 0:U], present[:, :, :].rearrange("p r e -> p (r e)"),
                       start=True, stop=True)
            for r in range(2):
                mm = eng.matmul(small_ps[0:EXPERTS, 16 + r * URANK:16 + (r + 1) * URANK], present[:, r, :],
                                ones[:, 0:URANK], start=True, stop=True)
            mm.then_inc(count_done, 1)
            eng.wait_ge(on_cols_ready, 1)
            eng.wait_ge(x1_done, PAIRS)
            eng.matmul(out_ps[0:U, 0:C], on_cols[:, :], b2_sb[:, :], start=True, stop=True).then_inc(bias_done, 1)
            eng.wait_ge(u_ready, 1)
            eng.wait_ge(rk_taken, PAIRS)
            eng.wait_ge(qk_taken, 2 * PAIRS)
            eng.wait_ge(v_taken, PAIRS)
            for n in range(4):
                for s in range(8):
                    mm = eng.transpose(bank[n][0:U, :].bitcast(BF16)[:, s * 128:(s + 1) * 128],
                                       u_tok[:, 8 * n + s, :], ident_bf[:, :])
                mm.then_inc(uT_done, 1)

            def coefs(i):
                for m in range(MT):
                    wait_apart(eng, mixed_done, MT * i + m - MT + 1)
                    eng.matmul(bank[m][:, :], spread[:, m * 128:(m + 1) * 128], u_sb[:, bass.ts(i, T)],
                               start=True, stop=True).then_inc(coef_done, 1)

            def second(i, par):
                wait_apart(eng, y_taken, i - 1)
                ps = hid_ps[par][0:C, :]
                eng.matmul(ps, bias_u[:, :], u_sb[:, bass.ts(i, T)], start=True, stop=False)
                for m in range(MT):
                    eng.wait_ge(mixed_done, MT * i + m + 1)
                    mm = eng.matmul(ps, w2T[:, m, :], h_mixed[par][:, m, :], start=False, stop=(m == MT - 1))
                mm.then_inc(y_done, 1)

            eng.wait_ge(spread_ready, 1)
            eng.wait_ge(u_taken, 4)
            coefs(0)
            eng.wait_ge(bias_ready, 1)
            eng.wait_ge(hid_free, MT * PAIRS + 2)
            coefs(1)
            second(0, 0)
            coefs(2)
            second(1, 1)
            with eng.Fori(1, PAIRS // 2 - 1) as k:
                coefs(2 * k + 1)
                second(2 * k, 0)
                coefs(2 * k + 2)
                second(2 * k + 1, 1)
            coefs(PAIRS - 1)
            second(PAIRS - 2, 0)
            second(PAIRS - 1, 1)

        @block.vector
        def _(eng):
            eng.sem_inc(logit_free, 1)

            def prep_scales():
                eng.wait_ge(in_w, 32)
                eng.tensor_reduce(max_w[:, :], wqkv_sb[:, :, :], AX.X, ALU.max, apply_absolute_value=True)
                eng.tensor_reduce(max_dw[:, :], wdw_sb[:, :, :], AX.X, ALU.max, apply_absolute_value=True)\
                   .then_inc(prep, 1)
                eng.wait_ge(prep, 1)
                eng.tensor_tensor(row_max[:, 0:2], max_w[:, 0:2], max_dw[:, 0:2], ALU.mult)
                eng.tensor_copy(row_max[:, 2:3], max_w[:, 2:3]).then_inc(prep, 1)
                eng.wait_ge(prep, 2)
                eng.tensor_scalar(row_max[:, :], row_max[:, :], TINY, 1.0 / W_SCALE, ALU.max, ALU.mult)\
                   .then_inc(prep, 1)
                eng.wait_ge(prep, 3)
                eng.reciprocal(row_scale[:, :], row_max[:, :]).then_inc(prep, 1)
                eng.wait_ge(prep, 4)
                eng.tensor_tensor(wqkv_scaled[:, :, :], wqkv_sb[:, :, :],
                                  row_scale[:, :].unsqueeze(2).broadcast_to([C, 3, C]), ALU.mult).then_inc(prep, 1)
                eng.tensor_scalar(v_taps[:, :], wdw_sb[:, 2, :], row_max[:, 2:3], 1.0 / X_SCALE,
                                  ALU.mult, ALU.mult).then_inc(prep, 1)

            def prep_weights():
                eng.wait_ge(wT_ready, 1)
                eng.wait_ge(in_dw, 16)
                for g in range(3):
                    taps = wdw_all[:, :].rearrange("p (o t) -> p t o", t=TAPS)[:, 3 * g:3 * g + 3, :]
                    eng.tensor_tensor(wc[:, 3 * g:3 * g + 3, :], taps,
                                      sc_ps[0:C, 0:QK].unsqueeze(1).broadcast_to([C, 3, QK]), ALU.mult)\
                       .then_inc(wc_full, 1)
                for g in range(3):
                    eng.wait_ge(wc_hi_set, g + 1)
                    eng.tensor_tensor(wc_lo[:, 3 * g:3 * g + 3, :], wc[:, 3 * g:3 * g + 3, :],
                                      wc_hi[:, 3 * g:3 * g + 3, :], ALU.subtract).then_inc(wc_lo_set, 1)
                    if g == 0:
                        eng.wait_ge(wv_set, 1)
                        eng.tensor_tensor(wv_lo[:, :], v_ps[0:C, 0:C], wv_hi[:, :], ALU.subtract)\
                           .then_inc(wv_set, 1)

            def prep_late():
                for b in range(2):
                    s = eng.tensor_scalar(floors[:, :, b], row_scale[:, 0:2], L2_EPS * X_SCALE, None, ALU.mult)
                s.then_inc(floors_set, 1)
                eng.wait_ge(floors_set, 1)
                eng.tensor_tensor(floors[:, :, :], floors[:, :, :], floors[:, :, :], ALU.mult).then_inc(floors_set, 1)
                eng.wait_ge(in_late, 16 * 8)
                eng.tensor_tensor(temp_own[:, :], temp_all[:, :],
                                  const("head", C).rearrange("p (h e) -> p h e", e=D)[:, :, 0], ALU.mult)\
                   .then_inc(temp_ready, 1)
                eng.wait_ge(temp_ready, 1)
                eng.tensor_reduce(temp_sb[:, :], temp_own[:, :], AX.X, ALU.add).then_inc(temp_ready, 1)
                eng.wait_ge(temp_ready, 2)
                eng.wait_ge(floors_set, 2)

            def channel_stats(i, nxt, moe):
                if nxt:
                    for b in range(2):
                        s = eng.bn_stats(stats[:, b, :], x_sb[:, i + 1, b * HW:(b + 1) * HW])
                if moe:
                    wait_apart(eng, x1_done, i - 1)
                    for b in range(2):
                        s = eng.bn_stats(stats[:, 2 + b, :], x_sb[:, i - 2, b * HW:(b + 1) * HW])
                if nxt or moe:
                    s.then_inc(stats_done, 1)
                else:
                    eng.sem_inc(stats_done, 1)
                wait_apart(eng, stats_done, i + 2)
                if isinstance(i, int) and i == -1:
                    eng.wait_ge(ones_set, 1)
                for b in ((0, 1) if nxt else ()) + ((2, 3) if moe else ()):
                    s = eng.bn_aggr(mv[:, b, :], stats[:, b, :])
                if nxt or moe:
                    s.then_inc(mv_ready, 1)
                else:
                    eng.sem_inc(mv_ready, 1)

            def low_parts(i, q):
                eng.wait_ge(hi_mid, i + 2)
                wait(eng, tile_done, 4 * i)
                if isinstance(i, int) and i <= 0:
                    eng.wait_ge(pads_set, i + 2)
                eng.tensor_tensor(inner(x_lo[q], 1), xs[q][:, :].rearrange("c (b h w) -> c b h w", b=2, w=W),
                                  inner(x_hi[q], 1), ALU.subtract).then_inc(lo_mid, 1)

            def turn(i, par, nxt, conv, att, moe, hid):
                q = 1 - par
                a, m = i - 1, i - 2
                if nxt:
                    wait_apart(eng, in_x[q], x_landed(i + 1, q))
                channel_stats(i, nxt, moe)
                if isinstance(i, int) and i == -1:
                    prep_scales()
                if isinstance(i, int) and i == 1:
                    prep_late()
                if att:
                    eng.wait_ge(gram_done, i)
                    eng.tensor_tensor(norm2[:, :], sc_ps[0:C, SQ:SQ + 4], floors[:, :, :].rearrange("p k b -> p (k b)"),
                                      ALU.max).then_inc(norm2_ready, 1)
                    eng.tensor_tensor(masked[:, :, :], sc_ps[0:C, 0:2 * C].rearrange("p (b e) -> p b e", b=2),
                                      const("head", C).unsqueeze(1).broadcast_to([C, 2, C]), ALU.mult)\
                       .then_inc(sm_step, 1)
                    eng.wait_ge(sm_step, SM * a + 1)
                    eng.tensor_reduce(picked[:, :, :], masked[:, :, :].rearrange("p b (h e) -> p b e h", h=HEADS),
                                      AX.X, ALU.add).then_inc(sm_step, 1)
                eng.wait_ge(mv_ready, i + 2)
                eng.wait_ge(dev_ready, i + 2)
                eng.tensor_tensor(var_dev[:, :], mv[:, :, 1], dev2[:, :], ALU.add).then_inc(vd_ready, 1)
                if att:
                    eng.wait_ge(rnorm_ready, i)
                    eng.tensor_tensor(k_diag[:, :, :], const("slot", C).unsqueeze(1).broadcast_to([C, 2, D]),
                                      rnorm[:, 2:4].unsqueeze(2).broadcast_to([C, 2, D]), ALU.mult)\
                       .then_inc(diag_ready, 1)
                    eng.tensor_scalar(q_fac[:, :], rnorm[:, 0:2], temp_sb[:, 0:1], None, ALU.mult)\
                       .then_inc(sm_step, 1)
                if conv:
                    taps(i, par, 0, 2)
                if att:
                    eng.wait_ge(rk_done, i)
                    eng.wait_ge(sm_step, SM * a + 3)
                    eng.tensor_tensor(sc_k[:, :, :], picked[:, :, :],
                                      sc_ps[0:C, RK:RK + 2 * D].rearrange("p (b e) -> p b e", b=2), ALU.mult)\
                       .then_inc(rk_taken, 1)
                    eng.wait_ge(rk_taken, i)
                    eng.tensor_tensor(sc_qk[:, :, :], sc_k[:, :, :], q_fac[:, :].unsqueeze(2).broadcast_to([C, 2, D]),
                                      ALU.mult).then_inc(sm_step, 1)
                    eng.wait_ge(sm_step, SM * a + 4)
                    eng.tensor_reduce(sc_max[:, :], sc_qk[:, :, :], AX.X, ALU.max).then_inc(sm_step, 1)
                    eng.wait_ge(sm_step, SM * a + 5)
                    eng.tensor_tensor(sc_in[:, :, :], sc_qk[:, :, :], sc_max[:, :].unsqueeze(2).broadcast_to([C, 2, D]),
                                      ALU.subtract).then_inc(sc_ready, 1)
                eng.wait_ge(var_ready, i + 2)
                eng.tensor_scalar(var_eps[:, :], small_ps[0:C, VAR:VAR + 4], GN_EPS, X_SCALE ** -2, ALU.add, ALU.mult)\
                   .then_inc(eps_ready, 1)
                if conv:
                    taps(i, par, 2, 3)
                if att:
                    eng.wait_ge(exp_ready, i)
                    eng.tensor_reduce(sc_sum[:, :], sc_exp[:, :, :], AX.X, ALU.add).then_inc(sm_step, 1)
                    eng.wait_ge(sm_step, SM * a + 6)
                    eng.reciprocal(sc_rec[:, :], sc_sum[:, :]).then_inc(sm_step, 1)
                    eng.wait_ge(sm_step, SM * a + 7)
                    eng.tensor_tensor(probs[:, :, :], sc_exp[:, :, :], sc_rec[:, :].unsqueeze(2).broadcast_to([C, 2, D]),
                                      ALU.mult).then_inc(sm_step, 1)
                    eng.wait_ge(sm_step, SM * a + 8)
                    wait(eng, mix_done, i - 1)
                    for b in range(2):
                        s = eng.tensor_tensor(attn[:, b, :].rearrange("p (h e) -> p h e", h=HEADS),
                                              probs[:, b, :].unsqueeze(1).broadcast_to([C, HEADS, D]),
                                              const("head", C).rearrange("p (h e) -> p h e", h=HEADS), ALU.mult)
                    s.then_inc(attn_ready, 1)
                eng.wait_ge(rstd_ready, i + 2)
                eng.scalar_tensor_tensor(out=shift[:, :], in0=small_ps[0:C, MEAN:MEAN + 4], scalar=-1.0,
                                         in1=rstd[:, :], op0=ALU.mult, op1=ALU.mult).then_inc(norm_done, 1)
                if conv:
                    taps(i, par, 3, 5)
                if nxt:
                    low_parts(i, q)
                if isinstance(i, int) and i == -1:
                    prep_weights()
                if conv:
                    taps(i, par, 5, 8)
                if att:
                    eng.wait_ge(out_done, i)
                    eng.tensor_tensor(x_sb[:, a, :], x_sb[:, a, :], out_ps[0:C, :], ALU.add).then_inc(x1_done, 1)
                if moe:
                    eng.wait_ge(gate_done, i - 1)
                    eng.scalar_tensor_tensor(
                        out=logits[:, m, :, :],
                        in0=small_ps[:, LOGIT:LOGIT + 4 * TILES].rearrange("p (t e) -> p t e", t=TILES),
                        scalar=1.0 / X_SCALE, in1=gate_b_sb[:, :].unsqueeze(1).broadcast_to([128, TILES, EXPERTS]),
                        op0=ALU.mult, op1=ALU.add).then_inc(logit_free, 1)

            SM = 8
            OUTER = [(dy, dx) for dy in (-1, 0, 1) for dx in (-1, 0, 1) if (dy, dx) != (0, 0)]

            def taps(i, par, lo, hi):
                if lo == 0:
                    eng.wait_ge(v_init, i + 1)
                for n in range(lo, hi):
                    dy, dx = OUTER[n]
                    t = 3 * (dy + 1) + dx + 1
                    wait(eng, tap_done, 8 * i + n)
                    eng.scalar_tensor_tensor(out=v_acc[par][:, :, :], in0=v_window(dy, dx), scalar=v_taps[:, t:t + 1],
                                             in1=v_acc[par][:, :, :], op0=ALU.mult, op1=ALU.add).then_inc(tap_done, 1)

            turns(eng, turn)

            steps = [0]

            def step(ins):
                steps[0] += 1
                ins.then_inc(g_step, 1)
                eng.wait_ge(g_step, steps[0])

            flat = logits[:, :, :, :].rearrange("p i t e -> p (i t) e")
            eng.wait_ge(logit_free, PAIRS + 1)
            step(eng.tensor_reduce(g_max[:, :], flat, AX.X, ALU.max))
            step(eng.tensor_tensor(g_in[:, :, :], flat, g_max[:, :].unsqueeze(2).broadcast_to([128, NT, EXPERTS]),
                                   ALU.subtract))
            eng.wait_ge(g_exp_ready, 1)
            step(eng.tensor_reduce(g_sum[:, :], g_exp[:, :, :], AX.X, ALU.add))
            step(eng.reciprocal(g_rec[:, :], g_sum[:, :]))
            step(eng.tensor_tensor(g_prob[:, :, :], g_exp[:, :, :],
                                   g_rec[:, :].unsqueeze(2).broadcast_to([128, NT, EXPERTS]), ALU.mult))
            every = [128, NT, EXPERTS, EXPERTS]
            score_j = g_prob[:, :, :].unsqueeze(2).broadcast_to(every)
            score_e = g_prob[:, :, :].unsqueeze(3).broadcast_to(every)
            step(eng.tensor_tensor(beats[:, :, :, :], score_j, score_e, ALU.is_gt))
            step(eng.tensor_tensor(ties[:, :, :].rearrange("p t (e j) -> p t e j", e=EXPERTS), score_j, score_e,
                                   ALU.is_equal))
            step(eng.tensor_tensor(beaten[:, :, :], ties[:, :, :],
                                   const("tri", 128).unsqueeze(1).broadcast_to([128, NT, 16]), ALU.mult))
            step(eng.tensor_tensor(beaten[:, :, :], beaten[:, :, :],
                                   beats[:, :, :, :].rearrange("p t e j -> p t (e j)"), ALU.add))
            step(eng.tensor_reduce(rank[:, :, :], beaten[:, :, :].rearrange("p t (e j) -> p t e j", e=EXPERTS),
                                   AX.X, ALU.add))
            eng.tensor_scalar(chosen[:, 0, :, :], rank[:, :, :], 0.0, None, ALU.is_equal)
            step(eng.tensor_scalar(chosen[:, 1, :, :], rank[:, :, :], 1.0, None, ALU.is_equal))
            eng.tensor_reduce(present[:, :, :], chosen[:, :, :, :].rearrange("p r t e -> p r e t"), AX.X, ALU.max)\
               .then_inc(present_ready, 1)
            step(eng.tensor_tensor(top_all[:, :, :, :].rearrange("p r t e -> p r (t e)"),
                                   chosen[:, :, :, :].rearrange("p r t e -> p r (t e)"),
                                   g_prob[:, :, :].rearrange("p t e -> p (t e)").unsqueeze(1)
                                   .broadcast_to([128, 2, NT * EXPERTS]), ALU.mult))
            step(eng.tensor_reduce(top[:, :, :], top_all[:, :, :, :], AX.X, ALU.add))
            step(eng.tensor_tensor(top_diff[:, :], top[:, 1, :], top[:, 0, :], ALU.subtract))
            assert steps[0] == TOP_DIFF
            eng.wait_ge(top_exp_ready, 1)
            step(eng.tensor_scalar(top_den[:, :], top_exp[:, :], 1.0, None, ALU.add))
            step(eng.reciprocal(top_w[:, 0, :], top_den[:, :]))
            step(eng.tensor_tensor(top_w[:, 1, :], top_exp[:, :], top_w[:, 0, :], ALU.mult))
            eng.tensor_copy(ident_bf[:, :], const("ident", 128))
            step(eng.tensor_copy(tw_hi[:, :, :], top_w[:, :, :]))
            step(eng.tensor_tensor(tw_rest[:, :, :], top_w[:, :, :], tw_hi[:, :, :], ALU.subtract))
            step(eng.tensor_copy(tw_mid[:, :, :], tw_rest[:, :, :]))
            step(eng.tensor_tensor(tw_lo[:, :, :], tw_rest[:, :, :], tw_mid[:, :, :], ALU.subtract))
            for part, at, n in ((tw_hi, 0, 3), (tw_mid, 3, 2), (tw_lo, 5, 1)):
                s = eng.tensor_copy(
                    u_tok[:, :, :].rearrange("p t (r u) -> p r t u", r=2)[:, :, :, at:at + n],
                    part[:, :, :].unsqueeze(3).broadcast_to([128, 2, NT, n]))
            s.then_inc(u_ready, 1)
            eng.wait_ge(count_done, 1)
            eng.tensor_scalar(on_cols[:, :], small_ps[0:EXPERTS, 16:16 + U], 1.0, None, ALU.min)\
               .then_inc(on_cols_ready, 1)
            step(eng.tensor_scalar(on_rows[:, :], small_ps[0:U, 0:2 * EXPERTS], 1.0, None, ALU.min))
            step(eng.tensor_scalar(spread0[:, :, :], on_rows[:, 0:EXPERTS].unsqueeze(2).broadcast_to([U, EXPERTS, C]),
                                   const("sel", U)[:, 0:1], None, ALU.mult))
            eng.scalar_tensor_tensor(out=spread[:, :].rearrange("p (e d) -> p e d", e=EXPERTS),
                                     in0=on_rows[:, EXPERTS:2 * EXPERTS].unsqueeze(2).broadcast_to([U, EXPERTS, C]),
                                     scalar=const("sel", U)[:, 1:2], in1=spread0[:, :, :],
                                     op0=ALU.mult, op1=ALU.add).then_inc(spread_ready, 1)
            eng.wait_ge(bias_done, 1)
            step(eng.tensor_copy(bias_hi[:, :], out_ps[0:U, 0:C]))
            step(eng.tensor_tensor(bias_rest[:, :], out_ps[0:U, 0:C], bias_hi[:, :], ALU.subtract))
            step(eng.tensor_copy(bias_mid[:, :], bias_rest[:, :]))
            step(eng.tensor_tensor(bias_lo[:, :], bias_rest[:, :], bias_mid[:, :], ALU.subtract))
            step(eng.tensor_scalar(bias_a[:, :], bias_hi[:, :], const("part", U)[:, 0:1], None, ALU.mult))
            step(eng.scalar_tensor_tensor(out=bias_b[:, :], in0=bias_mid[:, :], scalar=const("part", U)[:, 1:2],
                                          in1=bias_a[:, :], op0=ALU.mult, op1=ALU.add))
            eng.scalar_tensor_tensor(out=bias_u[:, :], in0=bias_lo[:, :], scalar=const("part", U)[:, 2:3],
                                     in1=bias_b[:, :], op0=ALU.mult, op1=ALU.add).then_inc(bias_ready, 1)

            eng.wait_ge(hid_free, MT * PAIRS + 2)

            def mix(i, par):
                wait(eng, y_done, i - 1)
                for m in range(MT):
                    eng.wait_ge(coef_done, MT * i + m + 1)
                    eng.tensor_tensor(h_mixed[par][:, m, :], hidden[:, i, m, :], bank[m][:, :], ALU.mult)\
                       .then_inc(mixed_done, 1)

            def add(i, par):
                eng.wait_ge(y_done, i + 1)
                wait(eng, stored[par], 8 * (i - par))
                eng.tensor_tensor(out_sb[par][:, :], x_sb[:, i, :], hid_ps[par][0:C, :], ALU.add)\
                   .then_inc(y_taken, 1)

            mix(0, 0)
            mix(1, 1)
            add(0, 0)
            mix(2, 0)
            add(1, 1)
            with eng.Fori(1, PAIRS // 2 - 1) as k:
                mix(2 * k + 1, 1)
                add(2 * k, 0)
                mix(2 * k + 2, 0)
                add(2 * k + 1, 1)
            mix(PAIRS - 1, 1)
            add(PAIRS - 2, 0)
            add(PAIRS - 1, 1)


def constants():
    import numpy as np
    c = np.arange(C)
    t = {n: np.zeros((128, w), np.float32) for n, w in CONSTS}
    t["ident"][:] = np.eye(128)
    same = (c[:, None] // GROUP == c[None, :] // GROUP) / GROUP
    t["avg"][:C] = same
    t["dev"][:C] = np.eye(C) - same
    t["head"][:C] = c[:, None] // D == c[None, :] // D
    t["slot"][:C] = c[:, None] % D == np.arange(D)[None, :]
    e = np.arange(EXPERTS)
    t["tri"][:] = (e[None, :] < e[:, None]).reshape(1, 16)
    bias_part = [0, 1, 2, 0, 1, 0]
    for k in range(U):
        t["sel"][k, k // URANK] = bias_part[k % URANK] == 0
        t["part"][k, bias_part[k % URANK]] = 1.0
    return np.concatenate([t[n] for n, _ in CONSTS], axis=1)


_INS = ["x", "L0_conv_w_qkv", "L0_conv_w_dw", "L0_conv_w_proj", "L0_conv_temperature", "L1_conv_gate_w",
        "L1_conv_gate_b", "L1_conv_w1", "L1_conv_b1", "L1_conv_w2", "L1_conv_b2"]


def kernel(**inputs):
    import numpy as np
    import concourse.bacc as bacc
    from concourse.bass_utils import run_bass_kernel_spmd

    nc = bacc.Bacc("TRN2", target_bir_lowering=False, num_devices=1)
    arrays, args = {}, []
    named = [(n, np.ascontiguousarray(inputs[n])) for n in _INS] + [("consts", constants())]
    for name, a in named:
        arrays[f"in_{name}"] = a
        args.append(nc.dram_tensor(f"in_{name}", a.shape, mybir.dt.from_np(a.dtype), kind="ExternalInput").ap())
    out = nc.dram_tensor("out_0", (B, C, H, W), F32, kind="ExternalOutput").ap()
    build(nc, *args, out)
    r = run_bass_kernel_spmd(nc, [arrays], core_ids=[0])
    return r.results[0]["out_0"]
```

```python
from contextlib import ExitStack

import concourse.bass as bass
from concourse import mybir

ALU = mybir.AluOpType
ACT = mybir.ActivationFunctionType
AX = mybir.AxisListType
F32 = mybir.dt.float32
F16 = mybir.dt.float16
BF16 = mybir.dt.bfloat16

B, C, H, W = 16, 96, 16, 16
HW = H * W
PAIRS = B // 2
T = 2 * HW
TILES = T // 128
TAPS = 9
HEADS = 8
D = C // HEADS
GROUP = C // 32
EXPERTS = 4
ED = EXPERTS * C
MT = ED // 128
QK = 2 * C
GN_EPS = 1e-5
L2_EPS = 1e-12
X_SCALE = 16.0
W_SCALE = 16.0
TINY = 1e-20
URANK = 6
U = 2 * URANK
VP = W + 1
VROWS = 2 * H + 1
PACKS = 6

CONSTS = [("ident", 128), ("avg", C), ("dev", C), ("head", C), ("slot", D), ("tri", 16),
          ("sel", 2), ("part", 3)]
CONST_AT = {}
_at = 0
for _n, _w in CONSTS:
    CONST_AT[_n] = (_at, _at + _w)
    _at += _w
CONST_W = _at


def build(nc, x, w_qkv, w_dw, w_proj, temperature, gate_w, gate_b, w1, b1, w2, b2, consts, out):
    ctx = ExitStack()
    with ctx:
        def sb(name, shape, dt=F32):
            return ctx.enter_context(nc.sbuf_tensor(name, shape, dt))

        def sem(name):
            return ctx.enter_context(nc.semaphore(name))

        cst = sb("cst", [128, CONST_W])

        def const(name, parts):
            a, b = CONST_AT[name]
            return cst[0:parts, a:b]

        wqkv_sb = sb("wqkv_sb", [C, 3, C])
        wdw_sb = sb("wdw_sb", [C, 3, TAPS])
        wdw_all = sb("wdw_all", [C, QK * TAPS])
        wproj_sb = sb("wproj_sb", [C, C])
        temp_all = sb("temp_all", [C, HEADS])
        temp_own = sb("temp_own", [C, HEADS])
        temp_sb = sb("temp_sb", [C, 1])
        gate_w_sb = sb("gate_w_sb", [C, EXPERTS])
        gate_b_sb = sb("gate_b_sb", [128, EXPERTS])
        w1_sb = sb("w1_sb", [128, MT, C])
        b1_sb = sb("b1_sb", [128, MT])
        w2_sb = sb("w2_sb", [C, ED])
        b2_sb = sb("b2_sb", [EXPERTS, C])
        ones = sb("ones", [128, 128])
        minus_half = sb("minus_half", [C, 4])
        max_w = sb("max_w", [C, 3])
        max_dw = sb("max_dw", [C, 3])
        row_max = sb("row_max", [C, 3])
        row_scale = sb("row_scale", [C, 3])
        wqkv_scaled = sb("wqkv_scaled", [C, 3, C])
        floors = sb("floors", [C, 2, 2])
        v_taps = sb("v_taps", [C, TAPS])
        wc = sb("wc", [C, TAPS, QK])
        w_a = sb("w_a", [128, TAPS, QK], F16)
        w_b = sb("w_b", [128, TAPS, QK], F16)
        w_c = sb("w_c", [C, 3, QK], F16)
        wv_hi = sb("wv_hi", [C, C], F16)
        wv_lo = sb("wv_lo", [C, C], F16)
        wprojT = sb("wprojT", [C, C])
        max_w1 = sb("max_w1", [128, MT])
        w1_row_max = sb("w1_row_max", [128, MT])
        w1_scale = sb("w1_scale", [128, MT])
        w1_scaled = sb("w1_scaled", [128, MT, C])
        w1_back = sb("w1_back", [128, MT])
        w1_hi = sb("w1_hi", [C, MT, 128], F16)
        w1_lo = sb("w1_lo", [C, MT, 128], F16)
        w2T = sb("w2T", [128, MT, C])

        x_sb = sb("x_sb", [C, PAIRS + 1, T])
        stats = sb("stats", [C, 4, 6])
        mv = sb("mv", [C, 4, 2])
        dev2 = sb("dev2", [C, 4])
        var_dev = sb("var_dev", [C, 4])
        var_eps = sb("var_eps", [C, 4])
        rstd = sb("rstd", [C, 4])
        shift = sb("shift", [C, 4])
        xs = [sb(f"xs{p}", [C, T]) for p in range(2)]
        grid = [3, 2, H + 2, W]
        x_a = [sb(f"x_a{p}", [128, *grid], F16) for p in range(2)]
        x_b = [sb(f"x_b{p}", [128, *grid], F16) for p in range(2)]
        x_c = [sb(f"x_c{p}", [C, *grid[1:]], F16) for p in range(2)]
        x_lo = [sb(f"x_lo{p}", [C, *grid], F16) for p in range(2)]
        v_grid = sb("v_grid", [C, (VROWS + 2) * VP + 2])
        v_acc = [sb(f"v_acc{p}", [C, VROWS, W]) for p in range(2)]
        qk_sb = sb("qk_sb", [128, TILES, QK])
        qk_sq = sb("qk_sq", [128, TILES, QK])
        sq_sum = sb("sq_sum", [128, 2, QK])
        masked = sb("masked", [C, 2, C])
        picked = sb("picked", [C, 2, D])
        norm2 = sb("norm2", [C, 4])
        rnorm = sb("rnorm", [C, 4])
        k_diag = sb("k_diag", [C, 2, D])
        q_fac = sb("q_fac", [C, 2])
        sc_k = sb("sc_k", [C, 2, D])
        sc_qk = sb("sc_qk", [C, 2, D])
        sc_max = sb("sc_max", [C, 2])
        sc_in = sb("sc_in", [C, 2, D])
        sc_exp = sb("sc_exp", [C, 2, D])
        sc_sum = sb("sc_sum", [C, 2])
        sc_rec = sb("sc_rec", [C, 2])
        probs = sb("probs", [C, 2, D])
        attn = sb("attn", [C, 2, C])
        mix_sb = sb("mix_sb", [C, 2, C])
        xn2 = [sb(f"xn2_{p}", [C, T]) for p in range(2)]
        xn2_hi = [sb(f"xn2_hi{p}", [C, T], F16) for p in range(2)]
        xn2_lo = [sb(f"xn2_lo{p}", [C, T], F16) for p in range(2)]
        hidden = sb("hidden", [128, PAIRS, MT, T])
        logits = sb("logits", [128, PAIRS, TILES, EXPERTS])
        NT = PAIRS * TILES
        EARLY = (PAIRS - 3) * TILES
        g_max = sb("g_max", [128, NT])
        g_in = sb("g_in", [128, NT, EXPERTS])
        g_exp = sb("g_exp", [128, NT, EXPERTS])
        g_sum = sb("g_sum", [128, NT])
        g_rec = sb("g_rec", [128, NT])
        g_prob = sb("g_prob", [128, NT, EXPERTS])
        beats = sb("beats", [128, NT, EXPERTS, EXPERTS])
        ties = sb("ties", [128, NT, 16])
        tied = sb("tied", [128, NT, 16])
        beaten = sb("beaten", [128, NT, 16])
        rank = sb("rank", [128, NT, EXPERTS])
        chosen = sb("chosen", [128, 2, NT, EXPERTS])
        present = sb("present", [128, 3, 2, EXPERTS])
        top_all = sb("top_all", [128, 2, NT, EXPERTS])
        top = sb("top", [128, 2, NT])
        top_diff = sb("top_diff", [128, NT])
        top_exp = sb("top_exp", [128, NT])
        top_den = sb("top_den", [128, NT])
        top_w = sb("top_w", [128, 2, NT])
        tw_hi = sb("tw_hi", [128, 2, NT], BF16)
        tw_rest = sb("tw_rest", [128, 2, NT])
        tw_mid = sb("tw_mid", [128, 2, NT], BF16)
        tw_lo = sb("tw_lo", [128, 2, NT], BF16)
        u_tok = sb("u_tok", [128, NT, U], BF16)
        ident_bf = sb("ident_bf", [128, 128], BF16)
        u_sb = sb("u_sb", [U, B * HW], BF16)
        on_rows = sb("on_rows", [U, 2 * EXPERTS])
        on_cols = sb("on_cols", [EXPERTS, U])
        spread0 = sb("spread0", [U, EXPERTS])
        spread1 = sb("spread1", [U, EXPERTS])
        spread = sb("spread", [U, ED], BF16)
        bias_hi = sb("bias_hi", [U, C], BF16)
        bias_rest = sb("bias_rest", [U, C])
        bias_mid = sb("bias_mid", [U, C], BF16)
        bias_lo = sb("bias_lo", [U, C], BF16)
        bias32 = sb("bias32", [U, C])
        bias_a = sb("bias_a", [U, C])
        bias_b = sb("bias_b", [U, C])
        bias_c = sb("bias_c", [U, C])
        bias_d = sb("bias_d", [U, C])
        bias_u = sb("bias_u", [U, C], BF16)
        h_mixed = [sb(f"h_mixed{p}", [128, MT, T]) for p in range(2)]
        out_sb = [sb(f"out_sb{p}", [C, T]) for p in range(2)]

        bank = [ctx.enter_context(nc.psum_tensor(f"bank{n}", [128, 512], F32)) for n in range(8)]
        qk_ps = bank[0:2]
        v_ps = bank[2]
        sc_ps = bank[3]
        small_ps = bank[4]
        out_ps = bank[5]
        hid_ps = [bank[2], bank[6], bank[7]]
        y_ps = bank[6:8]
        uT_bank = [sc_ps, out_ps, sc_ps, out_ps]
        MEAN, DEVI, VAR, MIX, LOGIT = 0, 4, 8, 16, 16 + QK
        SQ, RK = QK, QK + 4

        in_w = sem("in_w")
        in_dw = sem("in_dw")
        in_late = sem("in_late")
        in_x = [sem(f"in_x{i}") for i in range(3)]
        in_rest = sem("in_rest")
        ones_set = sem("ones_set")
        pads_set = sem("pads_set")
        prep = sem("prep")
        passed = sem("passed")
        wT_ready = sem("wT_ready")
        wc_full = sem("wc_full")
        wc_hi_set = sem("wc_hi_set")
        wc_lo_set = sem("wc_lo_set")
        wv_set = sem("wv_set")
        floors_set = sem("floors_set")
        in_c = sem("in_c")
        temp_ready = sem("temp_ready")
        late_T = sem("late_T")
        late_set = sem("late_set")
        x_stats_done = sem("x_stats_done")
        x1_stats_done = sem("x1_stats_done")
        mv_ready = sem("mv_ready")
        mean_ready = sem("mean_ready")
        dev_ready = sem("dev_ready")
        vd_ready = sem("vd_ready")
        var_ready = sem("var_ready")
        eps_ready = sem("eps_ready")
        rstd_ready = sem("rstd_ready")
        norm_done = sem("norm_done")
        xs_ready = sem("xs_ready")
        hi_mid = sem("hi_mid")
        hi_ready = sem("hi_ready")
        lo_mid = sem("lo_mid")
        lo_ready = sem("lo_ready")
        packed = [sem(f"packed{p}") for p in range(2)]
        w_packed = sem("w_packed")
        w1_step = sem("w1_step")
        v_ready = sem("v_ready")
        v_taken = sem("v_taken")
        v_init = sem("v_init")
        tap_done = sem("tap_done")
        tile_done = sem("tile_done")
        qk_taken = sem("qk_taken")
        gram_done = sem("gram_done")
        gram_taken = sem("gram_taken")
        norm2_ready = sem("norm2_ready")
        rnorm_ready = sem("rnorm_ready")
        sm_step = sem("sm_step")
        diag_ready = sem("diag_ready")
        rk_done = sem("rk_done")
        rk_taken = sem("rk_taken")
        sc_ready = sem("sc_ready")
        exp_ready = sem("exp_ready")
        attn_ready = sem("attn_ready")
        mix_done = sem("mix_done")
        mix_ready = sem("mix_ready")
        out_done = sem("out_done")
        x1_done = sem("x1_done")
        sq_ready = sem("sq_ready")
        xn2_ready = sem("xn2_ready")
        xn2_half_ready = sem("xn2_half_ready")
        xn2_hi_ready = sem("xn2_hi_ready")
        xn2_lo_ready = sem("xn2_lo_ready")
        gate_done = sem("gate_done")
        logit_free = sem("logit_free")
        hid_done = sem("hid_done")
        hid_free = sem("hid_free")
        g_step = sem("g_step")
        compared = sem("compared")
        g_in_ready = sem("g_in_ready")
        top_diff_ready = sem("top_diff_ready")
        bias_copied = sem("bias_copied")
        bias_step = sem("bias_step")
        g_exp_ready = sem("g_exp_ready")
        top_exp_ready = sem("top_exp_ready")
        present_ready = sem("present_ready")
        count_done = sem("count_done")
        on_cols_ready = sem("on_cols_ready")
        bias_done = sem("bias_done")
        spread_ready = sem("spread_ready")
        bias_ready = sem("bias_ready")
        u_ready = sem("u_ready")
        uT_done = sem("uT_done")
        u_taken = sem("u_taken")
        coef_done = sem("coef_done")
        mixed_done = sem("mixed_done")
        y_done = sem("y_done")
        y_taken = sem("y_taken")
        stored = [sem(f"stored{p}") for p in range(2)]

        x_dram = x.rearrange("(i b) c h w -> i c b (h w)", b=2)
        out_dram = out.rearrange("(i b) c h w -> i c b (h w)", b=2)

        def wait(eng, s, value):
            if not isinstance(value, int) or value > 0:
                eng.wait_ge(s, value)

        def wait_apart(eng, s, value):
            wait(eng, s, value)
            if not isinstance(value, int):
                eng.sem_inc(passed, 1)

        def i_is(i, value):
            return isinstance(i, int) and i == value

        def last_heads(i):
            return i_is(i, PAIRS)

        def chunk(c):
            return slice(0, EARLY) if c == 0 else slice(EARLY, NT)

        def pair_packed(pair, parity):
            return 8 * PACKS * (pair - parity) + 16 * PACKS

        def inner(t, dx):
            return t[0:C, dx, :, 1:H + 1, :]

        def window(t, half, dy):
            r = 8 * half + dy
            return t[:, r:r + 8, :].rearrange("c h w -> c (h w)")

        def turns(eng, turn):
            def short(i):
                turn(i, i % 2, i + 1 < PAIRS, 0 <= i < PAIRS, 0 <= i - 1 < PAIRS, 0 <= i - 2 < PAIRS,
                     0 <= i - 3 < PAIRS - 1)

            for i in range(-1, 3):
                short(i)
            with eng.Fori(1, 3) as k:
                turn(2 * k + 1, 1, True, True, True, True, True)
                turn(2 * k + 2, 0, True, True, True, True, True)
            for i in range(7, PAIRS + 2):
                short(i)

        def v_window(dy, dx):
            at = (1 + dy) * VP + 1 + dx
            return v_grid[:, at:at + VROWS * VP].rearrange("c (r w) -> c r w", w=VP)[:, :, 0:W]

        def gate_beaten(eng, c):
            t = chunk(c)
            eng.wait_ge(compared, 3 * c + 1)
            eng.tensor_tensor(tied[:, t, :], ties[:, t, :],
                              const("tri", 128).unsqueeze(1).broadcast_to([128, t.stop - t.start, 16]), ALU.mult)\
               .then_inc(compared, 1)
            eng.wait_ge(compared, 3 * c + 2)
            eng.tensor_tensor(beaten[:, t, :], tied[:, t, :],
                              beats[:, t, :, :].rearrange("p t e j -> p t (e j)"), ALU.add).then_inc(compared, 1)

        block = ctx.enter_context(nc.Block())

        @block.sync
        def _(eng):
            def load(i, landed):
                eng.dma_start(x_sb[:, i, :].rearrange("c (b t) -> c b t", b=2), x_dram[i]).then_inc(landed, 16)

            def pack(i, par):
                wait_apart(eng, hi_ready, i + 1)
                wait_apart(eng, tile_done, 4 * (i - 1))
                eng.dma_start(x_b[par][0:C], x_a[par][0:C]).then_inc(packed[par], 16)
                wait_apart(eng, lo_ready, i + 1)
                eng.dma_start(x_a[par][C:128], x_lo[par][0:32]).then_inc(packed[par], 16)
                eng.dma_start(x_b[par][C:128], x_lo[par][32:64]).then_inc(packed[par], 16)
                for dx in range(3):
                    eng.dma_start(x_c[par][32 * dx:32 * dx + 32], x_lo[par][64:C, dx]).then_inc(packed[par], 16)

            load(0, in_x[0])
            eng.dma_start(wqkv_sb[:, :, :], w_qkv.rearrange("(s o) c -> o s c", s=3)).then_inc(in_w, 16)
            eng.dma_start(wdw_sb[:, :, :], w_dw.rearrange("(s o) a b c -> o s (a b c)", s=3)).then_inc(in_w, 16)
            eng.dma_start(wdw_all[:, :], w_dw[0:QK].rearrange("o a b c -> (o a b c)").unsqueeze(0)
                          .broadcast_to([C, QK * TAPS])).then_inc(in_dw, 16)
            load(1, in_x[1])
            load(2, in_x[2])
            for dst, src in ((wproj_sb[:, :], w_proj), (gate_w_sb[:, :], gate_w),
                             (w1_sb[:, :, :], w1.rearrange("e d c -> (e d) c")
                              .rearrange("(m p) c -> p m c", p=128)),
                             (w2_sb[:, :].rearrange("p (e d) -> p e d", e=EXPERTS), w2.rearrange("e o d -> o e d")),
                             (b2_sb[:, :], b2),
                             (gate_b_sb[:, :], gate_b.unsqueeze(0).broadcast_to([128, EXPERTS])),
                             (temp_all[:, :], temperature.rearrange("a h b c -> a (h b c)").broadcast_to([C, HEADS]))):
                eng.dma_start(dst, src).then_inc(in_late, 16)
            eng.dma_start(b1_sb[:, :], b1.rearrange("e d -> (e d)").rearrange("(m p) -> p m", p=128),
                          allow_slow_non_contiguous=True).then_inc(in_late, 16)
            for i in range(3, PAIRS):
                load(i, in_rest)
            pack(0, 0)
            eng.wait_ge(wc_hi_set, 3)
            eng.dma_start(w_a[C:128, :, :], w_a[0:32, :, :]).then_inc(w_packed, 16)
            eng.dma_start(w_b[C:128, :, :], w_a[32:64, :, :]).then_inc(w_packed, 16)
            for dx in range(3):
                eng.dma_start(w_c[32 * dx:32 * dx + 32, :, :],
                              w_a[64:C, :, :].rearrange("c (y x) o -> c y x o", y=3)[:, :, dx, :]).then_inc(w_packed, 16)
            pack(1, 1)
            with eng.Fori(1, PAIRS // 2) as k:
                for p in range(2):
                    pack(2 * k + p, p)
            def store(i, p):
                eng.wait_ge(y_taken, i + 1)
                eng.dma_start(out_dram[i], out_sb[p][:, :].rearrange("c (b t) -> c b t", b=2)).then_inc(stored[p], 16)

            with eng.Fori(0, PAIRS // 2 - 1) as k:
                store(2 * k, 0)
                store(2 * k + 1, 1)
            store(PAIRS - 2, 0)
            for b in range(2):
                eng.wait_ge(y_taken, PAIRS + b)
                eng.dma_start(out_dram[PAIRS - 1][:, b, :], out_sb[1][:, b * HW:(b + 1) * HW]).then_inc(stored[1], 16)
            eng.wait_ge(stored[0], 16 * PAIRS // 2)
            eng.wait_ge(stored[1], 16 * (PAIRS // 2 + 1))

        @block.scalar
        def _(eng):
            eng.dma_start(cst[:, :], consts).then_inc(in_c, 16)
            eng.sem_inc(hid_free, 3)

            def copy_late():
                eng.wait_ge(late_T, 1)
                eng.copy(wprojT[:, :], out_ps[0:C, 0:C])
                eng.copy(w1_hi[:, :, :], hid_ps[1][0:C, 0:ED].rearrange("p (m d) -> p m d", m=MT))
                eng.copy(w2T[:, :, :], hid_ps[2][:, 0:MT * C].rearrange("p (m d) -> p m d", m=MT))\
                   .then_inc(late_set, 1)

            def high_weights(lo, hi):
                for g in range(lo, hi):
                    eng.wait_ge(wc_full, g + 1)
                    eng.copy(w_a[0:C, 3 * g:3 * g + 3, :], wc[:, 3 * g:3 * g + 3, :]).then_inc(wc_hi_set, 1)
                    if g == 0:
                        eng.copy(wv_hi[:, :], v_ps[0:C, 0:C]).then_inc(wv_set, 1)

            def take_v(i):
                eng.wait_ge(v_ready, i + 1)
                wait(eng, tap_done, 8 * i)
                if i_is(i, 0):
                    eng.wait_ge(pads_set, 1)
                grid = v_grid[:, VP:VP + 2 * (H + 1) * VP].rearrange(
                    "c (b h w) -> c b h w", b=2, w=VP)[:, :, 0:H, 1:W + 1]
                eng.copy(grid, v_ps[0:C, :].rearrange("c (b h w) -> c b h w", b=2, w=W)).then_inc(v_taken, 1)

            def centre_tap(i, par):
                eng.wait_ge(v_taken, i + 1)
                wait(eng, out_done, i - 1)
                if i_is(i, 0):
                    eng.wait_ge(prep, 6)
                eng.activation(v_acc[par][:, :, :], v_window(0, 0), ACT.Copy, scale=v_taps[:, 4:5])\
                   .then_inc(v_init, 1)

            def take_qk(i, b):
                eng.wait_ge(tile_done, TILES * i + 2 * b + 2)
                wait(eng, gram_done, i)
                src = qk_ps[b][:, 0:2 * QK].rearrange("p (t o) -> p t o", t=2)
                eng.copy(qk_sb[:, 2 * b:2 * b + 2, :], src)
                eng.activation(qk_sq[:, 2 * b:2 * b + 2, :], src, ACT.Square).then_inc(qk_taken, 1)

            def relu(m, lo, hi):
                for n in range(lo, hi):
                    eng.wait_ge(hid_done, MT * m + n + 1)
                    eng.activation(hidden[:, m, n, :], hid_ps[n][:, :], ACT.Relu,
                                   bias=b1_sb[:, n:n + 1], scale=w1_back[:, n:n + 1]).then_inc(hid_free, 1)

            def gate_exps(c):
                eng.wait_ge(g_in_ready, c + 1)
                eng.activation(g_exp[:, chunk(c), :], g_in[:, chunk(c), :], ACT.Exp).then_inc(g_exp_ready, 1)

            def top_exps(c):
                eng.wait_ge(top_diff_ready, c + 1)
                eng.activation(top_exp[:, chunk(c)], top_diff[:, chunk(c)], ACT.Exp).then_inc(top_exp_ready, 1)

            def turn(i, par, nxt, conv, att, moe, hid):
                q = 1 - par
                eng.wait_ge(mean_ready, i + 2)
                eng.activation(dev2[:, :], small_ps[0:C, DEVI:DEVI + 4], ACT.Square).then_inc(dev_ready, 1)
                if conv:
                    take_v(i)
                    centre_tap(i, par)
                if i_is(i, PAIRS - 1):
                    gate_exps(0)
                if last_heads(i):
                    relu(i - 4, 0, MT)
                    relu(i - 3, 0, 2)
                if nxt:
                    eng.wait_ge(norm_done, i + 2)
                    wait(eng, lo_mid, i)
                    for b in range(2):
                        a = eng.activation(xs[q][:, b * HW:(b + 1) * HW], x_sb[:, i + 1, b * HW:(b + 1) * HW],
                                           ACT.Identity, scale=rstd[:, b:b + 1], bias=shift[:, b:b + 1])
                    a.then_inc(xs_ready, 1)
                    eng.wait_ge(xs_ready, i + 2)
                    wait(eng, tile_done, 4 * i)
                    if isinstance(i, int) and i <= 0:
                        eng.wait_ge(pads_set, i + 2)
                    src = xs[q][:, :].rearrange("c (b h w) -> c b h w", b=2, w=W)
                    eng.copy(inner(x_a[q], 1), src).then_inc(hi_mid, 1)
                    if i_is(i, -1):
                        high_weights(0, 1)
                    eng.copy(inner(x_a[q], 0)[:, :, :, 1:W], src[:, :, :, 0:W - 1])
                    eng.copy(inner(x_a[q], 2)[:, :, :, 0:W - 1], src[:, :, :, 1:W]).then_inc(hi_ready, 1)
                if att:
                    eng.wait_ge(sc_ready, i)
                    eng.activation(sc_exp[:, :, :], sc_in[:, :, :], ACT.Exp).then_inc(exp_ready, 1)
                if i_is(i, -1):
                    high_weights(1, 3)
                elif nxt:
                    eng.wait_ge(lo_mid, i + 2)
                    src = inner(x_lo[q], 1)
                    eng.copy(inner(x_lo[q], 0)[:, :, :, 1:W], src[:, :, :, 0:W - 1])
                    eng.copy(inner(x_lo[q], 2)[:, :, :, 0:W - 1], src[:, :, :, 1:W]).then_inc(lo_ready, 1)
                if conv:
                    take_qk(i, 0)
                def xn2_half(b):
                    return eng.activation(xn2[par][:, b * HW:(b + 1) * HW], x_sb[:, i - 2, b * HW:(b + 1) * HW],
                                          ACT.Identity, scale=rstd[:, 2 + b:3 + b], bias=shift[:, 2 + b:3 + b])

                if moe:
                    eng.wait_ge(norm_done, i + 2)
                    wait(eng, hid_free, MT * (i - 4) + MT + 3)
                    xn2_half(0).then_inc(xn2_half_ready, 1)
                if last_heads(i):
                    relu(i - 3, 2, MT)
                if att:
                    eng.wait_ge(mix_done, i)
                    wait(eng, out_done, i - 1)
                    eng.copy(mix_sb[:, :, :], small_ps[0:C, MIX:MIX + QK].rearrange("p (b o) -> p b o", b=2))\
                       .then_inc(mix_ready, 1)
                if i_is(i, PAIRS - 1):
                    take_qk(i, 1)
                if moe:
                    xn2_half(1).then_inc(xn2_ready, 1)
                    eng.wait_ge(xn2_ready, i - 1)
                    eng.copy(xn2_hi[par][:, :], xn2[par][:, :]).then_inc(xn2_hi_ready, 1)
                if conv and not i_is(i, PAIRS - 1):
                    take_qk(i, 1)
                if i_is(i, 0):
                    copy_late()
                if last_heads(i):
                    top_exps(0)
                if hid and not last_heads(i) and not i_is(i, PAIRS - 1):
                    relu(i - 3, 0, 2 if i_is(i, PAIRS + 1) else MT)

            turns(eng, turn)

            def take_u(n):
                eng.wait_ge(uT_done, n + 1)
                eng.copy(u_sb[:, n * 1024:(n + 1) * 1024],
                         uT_bank[n][0:U, :].bitcast(BF16)[:, 0:1024]).then_inc(u_taken, 1)

            gate_exps(1)
            relu(PAIRS - 2, 2, MT)
            take_u(0)
            take_u(1)
            relu(PAIRS - 1, 0, MT)
            eng.wait_ge(bias_done, 1)
            eng.copy(bias32[:, :], out_ps[0:U, 0:C]).then_inc(bias_copied, 1)
            top_exps(1)
            take_u(2)
            take_u(3)

        @block.gpsimd
        def _(eng):
            eng.memset(mv[:, :, :], 1.0)
            eng.memset(rstd[:, :], 1.0)
            eng.memset(minus_half[:, :], -0.5).then_inc(ones_set, 1)
            eng.memset(x_sb[:, PAIRS, :], 0.0).then_inc(ones_set, 1)
            for p in range(2):
                for t in (x_a[p], x_lo[p]):
                    for row in (0, H + 1):
                        eng.memset(t[0:C, :, :, row, :], 0.0)
                    eng.memset(inner(t, 0)[:, :, :, 0:1], 0.0)
                    z = eng.memset(inner(t, 2)[:, :, :, W - 1:W], 0.0)
                if p == 0:
                    z = eng.memset(v_grid[:, :], 0.0)
                z.then_inc(pads_set, 1)
            eng.memset(ones[:, :], 1.0).then_inc(ones_set, 1)

            def low_parts(i, q):
                wait_apart(eng, hi_mid, i + 2)
                wait_apart(eng, tile_done, 4 * i)
                eng.tensor_tensor(inner(x_lo[q], 1), xs[q][:, :].rearrange("c (b h w) -> c b h w", b=2, w=W),
                                  inner(x_a[q], 1), ALU.subtract).then_inc(lo_mid, 1)

            def low_xn2(i, par):
                wait_apart(eng, xn2_hi_ready, i - 1)
                eng.tensor_tensor(xn2_lo[par][:, :], xn2[par][:, :], xn2_hi[par][:, :], ALU.subtract)\
                   .then_inc(xn2_lo_ready, 1)

            def head_rnorm(i):
                eng.wait_ge(norm2_ready, i)
                eng.tensor_tensor(rnorm[:, :], norm2[:, :], minus_half[:, :], ALU.pow).then_inc(rnorm_ready, 1)

            def turn(i, par, nxt, conv, att, moe, hid):
                q = 1 - par
                if att:
                    sq = qk_sq[:, :, :].rearrange("p (b h) o -> p b h o", b=2)
                    wait_apart(eng, qk_taken, 2 * i)
                    eng.tensor_tensor(sq_sum[:, :, :], sq[:, :, 0, :], sq[:, :, 1, :], ALU.add).then_inc(sq_ready, 1)
                if last_heads(i):
                    eng.wait_ge(in_c, 16)
                    gate_beaten(eng, 0)
                    low_xn2(i - 1, 1 - par)
                    head_rnorm(i)
                eng.wait_ge(eps_ready, i + 2)
                used = slice(0, 2) if i_is(i, -1) else slice(0 if conv else 2, 4)
                eng.tensor_tensor(rstd[:, used], var_eps[:, used], minus_half[:, used], ALU.pow)\
                   .then_inc(rstd_ready, 1)
                if att and not last_heads(i):
                    head_rnorm(i)
                if nxt:
                    low_parts(i, q)
                if moe and not i_is(i, PAIRS - 1):
                    low_xn2(i, par)

            turns(eng, turn)

            steps = [0]

            def step(ins):
                steps[0] += 1
                ins.then_inc(bias_step, 1)
                eng.wait_ge(bias_step, steps[0])

            def part(k):
                return const("part", U)[:, k:k + 1].broadcast_to([U, C])

            eng.wait_ge(bias_copied, 1)
            step(eng.tensor_copy(bias_hi[:, :], bias32[:, :]))
            step(eng.tensor_tensor(bias_rest[:, :], bias32[:, :], bias_hi[:, :], ALU.subtract))
            step(eng.tensor_copy(bias_mid[:, :], bias_rest[:, :]))
            step(eng.tensor_tensor(bias_lo[:, :], bias_rest[:, :], bias_mid[:, :], ALU.subtract))
            eng.tensor_tensor(bias_a[:, :], bias_hi[:, :], part(0), ALU.mult)
            eng.tensor_tensor(bias_b[:, :], bias_mid[:, :], part(1), ALU.mult)
            step(eng.tensor_tensor(bias_c[:, :], bias_lo[:, :], part(2), ALU.mult))
            step(eng.tensor_tensor(bias_d[:, :], bias_a[:, :], bias_b[:, :], ALU.add))
            eng.tensor_tensor(bias_u[:, :], bias_d[:, :], bias_c[:, :], ALU.add).then_inc(bias_ready, 1)

        @block.tensor
        def _(eng):
            def prepare_qkv():
                eng.wait_ge(prep, 5)
                for s in range(3):
                    to = sc_ps[0:C, s * C:(s + 1) * C] if s < 2 else v_ps[0:C, 0:C]
                    mm = eng.transpose(to, wqkv_scaled[:, s, :], const("ident", C)[:, 0:C])
                mm.then_inc(wT_ready, 1)

            def prepare_late():
                eng.wait_ge(w1_step, 4)
                eng.transpose(out_ps[0:C, 0:C], wproj_sb[:, :], const("ident", C)[:, 0:C])
                for m in range(MT):
                    eng.transpose(hid_ps[1][0:C, m * 128:(m + 1) * 128], w1_scaled[:, m, :], const("ident", 128))
                    mm = eng.transpose(hid_ps[2][:, m * C:(m + 1) * C], w2_sb[:, m * 128:(m + 1) * 128],
                                       const("ident", C)[:, 0:C])
                mm.then_inc(late_T, 1)

            def conv_taps(i, par, n, first, last):
                b, half = n // 2, n % 2
                if half == 0 and first == 0:
                    wait(eng, qk_taken, 2 * i + b - 1)
                ps = qk_ps[b][:, half * QK:(half + 1) * QK]
                if i_is(i, 0) or i_is(i, 1) and n == 0:
                    if n == 0 and first == 0:
                        eng.wait_ge(lo_ready, i + 1)
                    if n == TILES - 1 and first == 0:
                        eng.wait_ge(packed[par], pair_packed(i, par))
                    for t in range(first, last):
                        dy, dx = t // 3, t % 3
                        if i_is(i, 0) and n == 0 and dx == 0:
                            eng.wait_ge(wc_hi_set, dy + 1)
                            eng.wait_ge(wc_lo_set, dy + 1)
                        hi, lo = (window(x[par][0:C, dx, b], half, dy) for x in (x_a, x_lo))
                        eng.matmul(ps, hi, w_a[0:C, t, :], start=(t == 0), stop=False, skip_group_check=True)
                        eng.matmul(ps, hi, w_b[0:C, t, :], start=False, stop=False, skip_group_check=True)
                        mm = eng.matmul(ps, lo, w_a[0:C, t, :], start=False, stop=(t == TAPS - 1),
                                        skip_group_check=True)
                else:
                    if first == 0 and i_is(i, 1) and n == 1:
                        eng.wait_ge(w_packed, 16 * 5)
                    if first == 0 and n == (1 if i_is(i, 1) else 0):
                        eng.wait_ge(packed[par], pair_packed(i, par))
                    for t in range(first, last):
                        dy, dx = t // 3, t % 3
                        eng.matmul(ps, window(x_a[par][:, dx, b], half, dy), w_a[:, t, :], start=(t == 0), stop=False,
                                   skip_group_check=True)
                        mm = eng.matmul(ps, window(x_b[par][:, dx, b], half, dy), w_b[:, t, :], start=False,
                                        stop=False, skip_group_check=True)
                        if dx == 2:
                            mm = eng.matmul(ps, window(x_c[par][:, b], half, dy), w_c[:, dy, :], start=False,
                                            stop=(t == TAPS - 1), skip_group_check=True)
                if last == TAPS:
                    mm.then_inc(tile_done, 1)

            def keep_warm(n, ps=qk_ps[1]):
                for _ in range(n):
                    eng.matmul(ps[:, 0:128], ones[:, :], ones[:, :], start=True, stop=True)

            def norm_means(i):
                eng.wait_ge(mv_ready, i + 2)
                wait(eng, norm_done, i + 1)
                wait(eng, logit_free, i - 1)
                if i_is(i, -1):
                    eng.wait_ge(in_c, 16)
                    eng.wait_ge(ones_set, 3)
                eng.matmul(small_ps[0:C, MEAN:MEAN + 4], const("avg", C), mv[:, :, 0], start=True, stop=True)
                eng.matmul(small_ps[0:C, DEVI:DEVI + 4], const("dev", C), mv[:, :, 0], start=True, stop=True)\
                   .then_inc(mean_ready, 1)

            def norm_vars(i):
                eng.wait_ge(vd_ready, i + 2)
                eng.matmul(small_ps[0:C, VAR:VAR + 4], const("avg", C), var_dev[:, :], start=True, stop=True)\
                   .then_inc(var_ready, 1)

            def project_v(i, par):
                eng.wait_ge(hi_ready, i + 1)
                eng.wait_ge(lo_mid, i + 1)
                wait(eng, v_taken, i)
                wait(eng, hid_free, MT * (i - 4) + 4)
                if i_is(i, 0):
                    eng.wait_ge(wv_set, 2)
                for n, (wt, xt) in enumerate(((wv_hi, x_a), (wv_lo, x_a), (wv_hi, x_lo))):
                    mm = eng.matmul(v_ps[0:C, :], wt[:, :], inner(xt[par], 1), start=(n == 0), stop=(n == 2))
                mm.then_inc(v_ready, 1)

            def gram(i):
                eng.wait_ge(qk_taken, 2 * i)
                wait(eng, rk_taken, i - 1)
                for b in range(2):
                    for h in range(2):
                        eng.matmul(sc_ps[0:C, b * C:(b + 1) * C], qk_sb[:, 2 * b + h, 0:C],
                                   qk_sb[:, 2 * b + h, C:QK], start=(h == 0), stop=(h == 1))

            def norms(i):
                eng.wait_ge(sq_ready, i)
                if i_is(i, 1):
                    eng.wait_ge(ones_set, 3)
                for b in range(2):
                    for kind in range(2):
                        at = SQ + 2 * kind + b
                        mm = eng.matmul(sc_ps[0:C, at:at + 1], sq_sum[:, b, kind * C:(kind + 1) * C],
                                        ones[:, 0:1], start=True, stop=True)
                mm.then_inc(gram_done, 1)

            def spread_rk(i):
                eng.wait_ge(diag_ready, i)
                eng.matmul(sc_ps[0:C, RK:RK + 2 * D], const("head", C), k_diag[:, :, :].rearrange("p b e -> p (b e)"),
                           start=True, stop=True).then_inc(rk_done, 1)

            def mix_heads(i):
                eng.wait_ge(attn_ready, i)
                eng.wait_ge(norm_done, i + 2)
                if i_is(i, 1):
                    eng.wait_ge(late_set, 1)
                for b in range(2):
                    mm = eng.matmul(small_ps[0:C, MIX + b * C:MIX + (b + 1) * C], attn[:, b, :], wprojT[:, :],
                                    start=True, stop=True)
                mm.then_inc(mix_done, 1)

            def apply_mix(i, par):
                eng.wait_ge(mix_ready, i)
                eng.wait_ge(tap_done, 8 * i)
                wait(eng, x1_done, i - 1)
                for b in range(2):
                    mm = eng.matmul(out_ps[0:C, b * HW:(b + 1) * HW], mix_sb[:, b, :],
                                    v_acc[1 - par][:, b * (H + 1):b * (H + 1) + H, :].rearrange("c h w -> c (h w)"),
                                    start=True, stop=True)
                mm.then_inc(out_done, 1)

            def gate(i, par, att):
                eng.wait_ge(xn2_half_ready, i - 1)
                if att:
                    eng.wait_ge(mix_ready, i)
                else:
                    eng.wait_ge(norm_done, i + 2)
                for t in range(TILES):
                    if t == TILES // 2:
                        eng.wait_ge(xn2_ready, i - 1)
                    mm = eng.matmul(small_ps[:, LOGIT + 4 * t:LOGIT + 4 * t + 4], xn2[par][:, t * 128:(t + 1) * 128],
                                    gate_w_sb[:, :], start=True, stop=True)
                mm.then_inc(gate_done, 1)

            def first(m, par, lo, hi, v_count):
                for n in range(lo, hi):
                    eng.wait_ge(hid_free, MT * m + n + 1)
                    if n == 0:
                        if isinstance(m, int) and m == 0:
                            eng.wait_ge(w1_step, 5)
                        wait(eng, v_taken, v_count)
                        eng.wait_ge(xn2_lo_ready, m + 1)
                    ps = hid_ps[n][:, :]
                    eng.matmul(ps, w1_hi[:, n, :], xn2_hi[par][:, :], start=True, stop=False)
                    eng.matmul(ps, w1_lo[:, n, :], xn2_hi[par][:, :], start=False, stop=False)
                    eng.matmul(ps, w1_hi[:, n, :], xn2_lo[par][:, :], start=False, stop=True).then_inc(hid_done, 1)

            def turn(i, par, nxt, conv, att, moe, hid):
                if conv:
                    project_v(i, par)
                if att:
                    gram(i)
                if i_is(i, 0):
                    conv_taps(i, par, 0, 0, TAPS)
                if last_heads(i):
                    first(i - 4, par, 0, 2, PAIRS)
                norm_means(i)
                if conv and not i_is(i, 0):
                    conv_taps(i, par, 0, 0, 3)
                if att:
                    norms(i)
                if last_heads(i):
                    first(i - 4, par, 2, MT, 0)
                    keep_warm(1)
                if i_is(i, PAIRS + 1):
                    first(i - 3, 1 - par, 0, 1, PAIRS)
                if i_is(i, 0):
                    conv_taps(i, par, 1, 0, 3)
                norm_vars(i)
                if conv and not i_is(i, 0):
                    conv_taps(i, par, 0, 3, TAPS)
                if conv:
                    conv_taps(i, par, 1, 3 if i_is(i, 0) else 0, TAPS)
                    conv_taps(i, par, 2, 0, 3)
                if last_heads(i):
                    first(i - 3, 1 - par, 0, 2, PAIRS)
                    keep_warm(3)
                if att:
                    spread_rk(i)
                if last_heads(i):
                    first(i - 3, 1 - par, 2, MT, 0)
                    keep_warm(6)
                if conv:
                    conv_taps(i, par, 2, 3, TAPS)
                    conv_taps(i, par, 3, 0, TAPS)
                if i_is(i, -1):
                    keep_warm(3)
                    prepare_qkv()
                    keep_warm(6)
                if i_is(i, 0):
                    prepare_late()
                hid_here = hid and conv and not i_is(i, PAIRS - 1)
                if hid_here:
                    first(i - 3, 1 - par, 0, 2, i + 1)
                if i_is(i, PAIRS + 1):
                    first(i - 3, 1 - par, 1, MT, 0)
                    keep_warm(6)
                if att:
                    mix_heads(i)
                if last_heads(i):
                    keep_warm(2)
                if hid_here:
                    first(i - 3, 1 - par, 2, MT, 0)
                if att:
                    apply_mix(i, par)
                if moe:
                    gate(i, par, att)
                if last_heads(i):
                    keep_warm(4)

            turns(eng, turn)

            def turn_u(n):
                for s in range(8):
                    mm = eng.transpose(uT_bank[n][0:U, :].bitcast(BF16)[:, s * 128:(s + 1) * 128],
                                       u_tok[:, 8 * n + s, :], ident_bf[:, :])
                mm.then_inc(uT_done, 1)

            eng.wait_ge(u_ready, 1)
            eng.wait_ge(rk_taken, PAIRS)
            eng.wait_ge(x1_done, PAIRS)
            turn_u(0)
            turn_u(1)
            first(PAIRS - 1, 1, 0, 2, PAIRS)
            keep_warm(5)

            eng.wait_ge(present_ready, 1)
            eng.wait_ge(logit_free, PAIRS + 1)
            both = present[:, 2, :, :]
            eng.matmul(small_ps[0:U, 0:2 * EXPERTS], ones[:, 0:U], both.rearrange("p r e -> p (r e)"),
                       start=True, stop=True)
            for r in range(2):
                mm = eng.matmul(small_ps[0:EXPERTS, 16 + r * URANK:16 + (r + 1) * URANK], both[:, r, :],
                                ones[:, 0:URANK], start=True, stop=True)
            mm.then_inc(count_done, 1)
            first(PAIRS - 1, 1, 2, MT, 0)
            eng.wait_ge(on_cols_ready, 1)
            eng.wait_ge(u_taken, 2)
            eng.matmul(out_ps[0:U, 0:C], on_cols[:, :], b2_sb[:, :], start=True, stop=True).then_inc(bias_done, 1)
            keep_warm(3)

            def coef(i, m):
                wait_apart(eng, mixed_done, MT * i + m - MT + 1)
                eng.matmul(bank[m][:, :], spread[:, m * 128:(m + 1) * 128], u_sb[:, bass.ts(i, T)],
                           start=True, stop=True).then_inc(coef_done, 1)

            def last_second(i, par):
                eng.wait_ge(y_taken, i - 1)
                eng.wait_ge(mixed_done, MT * i + MT)
                for b in range(2):
                    t = slice(b * HW, (b + 1) * HW)
                    ps = y_ps[par if b == 0 else 1 - par][0:C, t]
                    if b == 1:
                        eng.wait_ge(y_taken, i)
                    for m in range(MT):
                        eng.matmul(ps, w2T[:, m, :], h_mixed[par][:, m, t], start=(m == 0), stop=False)
                    eng.matmul(ps, bias_u[:, :], u_sb[:, i * T + b * HW:i * T + (b + 1) * HW], start=False, stop=True)\
                       .then_inc(y_done, 1)

            def second(i, par):
                wait_apart(eng, y_taken, i - 1)
                ps = y_ps[par][0:C, :]
                for m in range(MT):
                    coef(i + 1, m)
                    eng.wait_ge(mixed_done, MT * i + m + 1)
                    eng.matmul(ps, w2T[:, m, :], h_mixed[par][:, m, :], start=(m == 0), stop=False,
                               skip_group_check=True)
                if i_is(i, 0):
                    eng.wait_ge(bias_ready, 1)
                eng.matmul(ps, bias_u[:, :], u_sb[:, bass.ts(i, T)], start=False, stop=True,
                           skip_group_check=True).then_inc(y_done, 1)

            eng.wait_ge(spread_ready, 1)
            eng.wait_ge(qk_taken, 2 * PAIRS)
            eng.wait_ge(hid_free, MT * PAIRS + 1)
            for m in range(MT):
                coef(0, m)
            eng.wait_ge(hid_free, MT * PAIRS + 3)
            keep_warm(3, y_ps[0])
            second(0, 0)
            second(1, 1)
            eng.wait_ge(u_ready, 2)
            eng.wait_ge(bias_copied, 1)
            turn_u(2)
            turn_u(3)
            second(2, 0)
            eng.wait_ge(u_taken, 4)
            with eng.Fori(1, PAIRS // 2 - 1) as k:
                second(2 * k + 1, 1)
                second(2 * k + 2, 0)
            last_second(PAIRS - 1, 1)

        @block.vector
        def _(eng):
            eng.sem_inc(logit_free, 1)

            def prep_scales():
                eng.wait_ge(in_w, 32)
                eng.tensor_reduce(max_w[:, :], wqkv_sb[:, :, :], AX.X, ALU.max, apply_absolute_value=True)
                eng.tensor_reduce(max_dw[:, :], wdw_sb[:, :, :], AX.X, ALU.max, apply_absolute_value=True)\
                   .then_inc(prep, 1)

            def combine_scales():
                eng.wait_ge(prep, 1)
                eng.tensor_tensor(row_max[:, 0:2], max_w[:, 0:2], max_dw[:, 0:2], ALU.mult)
                eng.tensor_copy(row_max[:, 2:3], max_w[:, 2:3]).then_inc(prep, 1)
                eng.wait_ge(prep, 2)
                eng.tensor_scalar(row_max[:, :], row_max[:, :], TINY, 1.0 / W_SCALE, ALU.max, ALU.mult)\
                   .then_inc(prep, 1)
                eng.wait_ge(prep, 3)
                eng.reciprocal(row_scale[:, :], row_max[:, :]).then_inc(prep, 1)

            def scale_weights():
                eng.wait_ge(prep, 4)
                eng.tensor_tensor(wqkv_scaled[:, :, :], wqkv_sb[:, :, :],
                                  row_scale[:, :].unsqueeze(2).broadcast_to([C, 3, C]), ALU.mult).then_inc(prep, 1)
                eng.tensor_scalar(v_taps[:, :], wdw_sb[:, 2, :], row_max[:, 2:3], 1.0 / X_SCALE,
                                  ALU.mult, ALU.mult).then_inc(prep, 1)

            def combine(g):
                taps = wdw_all[:, :].rearrange("p (o t) -> p t o", t=TAPS)[:, 3 * g:3 * g + 3, :]
                eng.tensor_tensor(wc[:, 3 * g:3 * g + 3, :], taps,
                                  sc_ps[0:C, 0:QK].unsqueeze(1).broadcast_to([C, 3, QK]), ALU.mult)\
                   .then_inc(wc_full, 1)

            def low_weights(g):
                eng.wait_ge(wc_hi_set, g + 1)
                eng.tensor_tensor(w_b[0:C, 3 * g:3 * g + 3, :], wc[:, 3 * g:3 * g + 3, :],
                                  w_a[0:C, 3 * g:3 * g + 3, :], ALU.subtract).then_inc(wc_lo_set, 1)

            def prep_weights(q):
                eng.wait_ge(wT_ready, 1)
                eng.wait_ge(in_dw, 16)
                combine(0)
                combine(1)
                low_weights(0)
                eng.wait_ge(wv_set, 1)
                eng.tensor_tensor(wv_lo[:, :], v_ps[0:C, 0:C], wv_hi[:, :], ALU.subtract).then_inc(wv_set, 1)
                eng.wait_ge(lo_mid, 1)
                src = inner(x_lo[q], 1)
                eng.tensor_copy(inner(x_lo[q], 0)[:, :, :, 1:W], src[:, :, :, 0:W - 1])
                eng.tensor_copy(inner(x_lo[q], 2)[:, :, :, 0:W - 1], src[:, :, :, 1:W]).then_inc(lo_ready, 1)
                combine(2)
                low_weights(1)
                low_weights(2)

            def prep_w1():
                eng.wait_ge(in_late, 16 * 8)
                eng.tensor_reduce(max_w1[:, :], w1_sb[:, :, :], AX.X, ALU.max, apply_absolute_value=True)\
                   .then_inc(w1_step, 1)
                eng.wait_ge(w1_step, 1)
                eng.tensor_scalar(w1_row_max[:, :], max_w1[:, :], TINY, 1.0 / W_SCALE, ALU.max, ALU.mult)\
                   .then_inc(w1_step, 1)
                eng.wait_ge(w1_step, 2)
                eng.tensor_scalar(w1_back[:, :], w1_row_max[:, :], 1.0 / X_SCALE, None, ALU.mult)
                eng.reciprocal(w1_scale[:, :], w1_row_max[:, :]).then_inc(w1_step, 1)
                eng.wait_ge(w1_step, 3)
                eng.tensor_tensor(w1_scaled[:, :, :], w1_sb[:, :, :],
                                  w1_scale[:, :].unsqueeze(2).broadcast_to([128, MT, C]), ALU.mult)\
                   .then_inc(w1_step, 1)

            def prep_late():
                for b in range(2):
                    s = eng.tensor_scalar(floors[:, :, b], row_scale[:, 0:2], L2_EPS * X_SCALE, None, ALU.mult)
                s.then_inc(floors_set, 1)
                eng.wait_ge(floors_set, 1)
                eng.tensor_tensor(floors[:, :, :], floors[:, :, :], floors[:, :, :], ALU.mult).then_inc(floors_set, 1)
                eng.tensor_tensor(temp_own[:, :], temp_all[:, :],
                                  const("head", C).rearrange("p (h e) -> p h e", e=D)[:, :, 0], ALU.mult)\
                   .then_inc(temp_ready, 1)
                eng.wait_ge(temp_ready, 1)
                eng.tensor_reduce(temp_sb[:, :], temp_own[:, :], AX.X, ALU.add).then_inc(temp_ready, 1)
                eng.wait_ge(temp_ready, 2)
                eng.wait_ge(floors_set, 2)
                eng.tensor_copy(ident_bf[:, :], const("ident", 128))

            def x_stats(j):
                for b in range(2):
                    s = eng.bn_stats(stats[:, b, :], x_sb[:, j, b * HW:(b + 1) * HW])
                s.then_inc(x_stats_done, 1)

            def x1_stats(j):
                wait_apart(eng, x1_done, j + 1)
                for b in range(2):
                    s = eng.bn_stats(stats[:, 2 + b, :], x_sb[:, j, b * HW:(b + 1) * HW])
                s.then_inc(x1_stats_done, 1)

            def channel_means(i, nxt, moe):
                if nxt:
                    wait_apart(eng, x_stats_done, i + 2)
                if moe:
                    wait_apart(eng, x1_stats_done, i - 1)
                for b in ((0, 1) if nxt else ()) + ((2, 3) if moe else ()):
                    s = eng.bn_aggr(mv[:, b, :], stats[:, b, :])
                s.then_inc(mv_ready, 1)

            steps = [0]

            def step(ins):
                steps[0] += 1
                ins.then_inc(g_step, 1)
                eng.wait_ge(g_step, steps[0])

            def gate_logits(c):
                t = chunk(c)
                flat = logits[:, :, :, :].rearrange("p i t e -> p (i t) e")[:, t, :]
                eng.wait_ge(logit_free, PAIRS - 2 if c == 0 else PAIRS + 1)
                step(eng.tensor_reduce(g_max[:, t], flat, AX.X, ALU.max))
                eng.tensor_tensor(g_in[:, t, :], flat, g_max[:, t].unsqueeze(2).broadcast_to(list(flat.shape)),
                                  ALU.subtract).then_inc(g_in_ready, 1)

            def gate_compare(c):
                t = chunk(c)
                every = [128, t.stop - t.start, EXPERTS, EXPERTS]
                score_j = g_exp[:, t, :].unsqueeze(2).broadcast_to(every)
                score_e = g_exp[:, t, :].unsqueeze(3).broadcast_to(every)
                eng.wait_ge(g_exp_ready, c + 1)
                eng.tensor_tensor(beats[:, t, :, :], score_j, score_e, ALU.is_gt)
                eng.tensor_tensor(ties[:, t, :].rearrange("p t (e j) -> p t e j", e=EXPERTS), score_j, score_e,
                                  ALU.is_equal).then_inc(compared, 1)

            def gate_rank(c):
                t = chunk(c)
                eng.wait_ge(compared, 3 * c + 3)
                step(eng.tensor_reduce(rank[:, t, :], beaten[:, t, :].rearrange("p t (e j) -> p t e j", e=EXPERTS),
                                       AX.X, ALU.add))

            def gate_present(c):
                t = chunk(c)
                eng.tensor_scalar(chosen[:, 0, t, :], rank[:, t, :], 0.0, None, ALU.is_equal)
                step(eng.tensor_scalar(chosen[:, 1, t, :], rank[:, t, :], 1.0, None, ALU.is_equal))
                step(eng.tensor_reduce(present[:, c, :, :], chosen[:, :, t, :].rearrange("p r t e -> p r e t"),
                                       AX.X, ALU.max))
                if c == 1:
                    eng.tensor_tensor(present[:, 2, :, :], present[:, 0, :, :], present[:, 1, :, :], ALU.max)\
                       .then_inc(present_ready, 1)

            def gate_scores(c):
                t = chunk(c)
                n = t.stop - t.start
                step(eng.tensor_reduce(g_sum[:, t], g_exp[:, t, :], AX.X, ALU.add))
                step(eng.reciprocal(g_rec[:, t], g_sum[:, t]))
                step(eng.tensor_tensor(g_prob[:, t, :], g_exp[:, t, :],
                                       g_rec[:, t].unsqueeze(2).broadcast_to([128, n, EXPERTS]), ALU.mult))
                step(eng.tensor_tensor(top_all[:, :, t, :], chosen[:, :, t, :],
                                       g_prob[:, t, :].unsqueeze(1).broadcast_to([128, 2, n, EXPERTS]), ALU.mult))
                step(eng.tensor_reduce(top[:, :, t], top_all[:, :, t, :], AX.X, ALU.add))
                eng.tensor_tensor(top_diff[:, t], top[:, 1, t], top[:, 0, t], ALU.subtract).then_inc(top_diff_ready, 1)

            def gate_weights(c):
                t = chunk(c)
                eng.wait_ge(top_exp_ready, c + 1)
                step(eng.tensor_scalar(top_den[:, t], top_exp[:, t], 1.0, None, ALU.add))
                step(eng.reciprocal(top_w[:, 0, t], top_den[:, t]))
                step(eng.tensor_tensor(top_w[:, 1, t], top_exp[:, t], top_w[:, 0, t], ALU.mult))

            def gate_parts(c):
                t = chunk(c)
                n = t.stop - t.start
                step(eng.tensor_copy(tw_hi[:, :, t], top_w[:, :, t]))
                step(eng.tensor_tensor(tw_rest[:, :, t], top_w[:, :, t], tw_hi[:, :, t], ALU.subtract))
                step(eng.tensor_copy(tw_mid[:, :, t], tw_rest[:, :, t]))
                step(eng.tensor_tensor(tw_lo[:, :, t], tw_rest[:, :, t], tw_mid[:, :, t], ALU.subtract))
                for part, at, k in ((tw_hi, 0, 3), (tw_mid, 3, 2), (tw_lo, 5, 1)):
                    s = eng.tensor_copy(
                        u_tok[:, t, :].rearrange("p t (r u) -> p r t u", r=2)[:, :, :, at:at + k],
                        part[:, :, t].unsqueeze(3).broadcast_to([128, 2, n, k]))
                s.then_inc(u_ready, 1)

            def head_factors(i):
                eng.wait_ge(rnorm_ready, i)
                eng.tensor_tensor(k_diag[:, :, :], const("slot", C).unsqueeze(1).broadcast_to([C, 2, D]),
                                  rnorm[:, 2:4].unsqueeze(2).broadcast_to([C, 2, D]), ALU.mult)\
                   .then_inc(diag_ready, 1)
                eng.tensor_scalar(q_fac[:, :], rnorm[:, 0:2], temp_sb[:, 0:1], None, ALU.mult)\
                   .then_inc(sm_step, 1)

            def turn(i, par, nxt, conv, att, moe, hid):
                q = 1 - par
                a, m = i - 1, i - 2
                if att:
                    taps(a, q, 6, 7)
                if i_is(i, -1):
                    prep_scales()
                eng.wait_ge(mv_ready, i + 2)
                eng.wait_ge(dev_ready, i + 2)
                eng.tensor_tensor(var_dev[:, :], mv[:, :, 1], dev2[:, :], ALU.add).then_inc(vd_ready, 1)
                if att:
                    taps(a, q, 7, 8)
                if i_is(i, 1):
                    prep_late()
                    eng.wait_ge(late_set, 1)
                    eng.tensor_tensor(w1_lo[:, :, :], hid_ps[1][0:C, 0:ED].rearrange("p (m d) -> p m d", m=MT),
                                      w1_hi[:, :, :], ALU.subtract).then_inc(w1_step, 1)
                if att:
                    eng.wait_ge(gram_done, i)
                    eng.tensor_tensor(norm2[:, :], sc_ps[0:C, SQ:SQ + 4], floors[:, :, :].rearrange("p k b -> p (k b)"),
                                      ALU.max).then_inc(norm2_ready, 1)
                    eng.tensor_tensor(masked[:, :, :], sc_ps[0:C, 0:2 * C].rearrange("p (b e) -> p b e", b=2),
                                      const("head", C).unsqueeze(1).broadcast_to([C, 2, C]), ALU.mult)\
                       .then_inc(sm_step, 1)
                    eng.wait_ge(sm_step, SM * a + 1)
                    eng.tensor_reduce(picked[:, :, :], masked[:, :, :].rearrange("p b (h e) -> p b e h", h=HEADS),
                                      AX.X, ALU.add).then_inc(sm_step, 1)
                eng.wait_ge(var_ready, i + 2)
                eng.tensor_scalar(var_eps[:, :], small_ps[0:C, VAR:VAR + 4], GN_EPS, X_SCALE ** -2, ALU.add, ALU.mult)\
                   .then_inc(eps_ready, 1)
                if i_is(i, PAIRS - 1):
                    gate_logits(0)
                if last_heads(i):
                    gate_rank(0)
                if i_is(i, -1):
                    combine_scales()
                if conv:
                    taps(i, par, 0, 1)
                if last_heads(i):
                    head_factors(i)
                eng.wait_ge(rstd_ready, i + 2)
                eng.scalar_tensor_tensor(out=shift[:, :], in0=small_ps[0:C, MEAN:MEAN + 4], scalar=-1.0,
                                         in1=rstd[:, :], op0=ALU.mult, op1=ALU.mult).then_inc(norm_done, 1)
                if i_is(i, -1):
                    scale_weights()
                if i_is(i, PAIRS + 1):
                    gate_parts(0)
                if conv:
                    taps(i, par, 1, 2)
                if att and not last_heads(i):
                    head_factors(i)
                if conv:
                    taps(i, par, 2, 3)
                if att:
                    eng.wait_ge(rk_done, i)
                    eng.wait_ge(sm_step, SM * a + 3)
                    eng.tensor_tensor(sc_k[:, :, :], picked[:, :, :],
                                      sc_ps[0:C, RK:RK + 2 * D].rearrange("p (b e) -> p b e", b=2), ALU.mult)\
                       .then_inc(rk_taken, 1)
                    eng.wait_ge(rk_taken, i)
                    eng.tensor_tensor(sc_qk[:, :, :], sc_k[:, :, :], q_fac[:, :].unsqueeze(2).broadcast_to([C, 2, D]),
                                      ALU.mult).then_inc(sm_step, 1)
                    eng.wait_ge(sm_step, SM * a + 4)
                    eng.tensor_reduce(sc_max[:, :], sc_qk[:, :, :], AX.X, ALU.max).then_inc(sm_step, 1)
                    eng.wait_ge(sm_step, SM * a + 5)
                    eng.tensor_tensor(sc_in[:, :, :], sc_qk[:, :, :], sc_max[:, :].unsqueeze(2).broadcast_to([C, 2, D]),
                                      ALU.subtract).then_inc(sc_ready, 1)
                if i_is(i, -1):
                    prep_weights(q)
                if isinstance(i, int) and i <= 0:
                    eng.wait_ge(in_x[i + 2], 16)
                if i_is(i, 1):
                    eng.wait_ge(in_rest, 16 * (PAIRS - 3))
                ahead = not isinstance(i, int) or i + 2 < PAIRS
                if ahead:
                    x_stats(i + 2)
                if i_is(i, 0):
                    prep_w1()
                if att:
                    eng.wait_ge(exp_ready, i)
                    eng.tensor_reduce(sc_sum[:, :], sc_exp[:, :, :], AX.X, ALU.add).then_inc(sm_step, 1)
                    eng.wait_ge(sm_step, SM * a + 6)
                    eng.reciprocal(sc_rec[:, :], sc_sum[:, :]).then_inc(sm_step, 1)
                    eng.wait_ge(sm_step, SM * a + 7)
                    eng.tensor_tensor(probs[:, :, :], sc_exp[:, :, :], sc_rec[:, :].unsqueeze(2).broadcast_to([C, 2, D]),
                                      ALU.mult).then_inc(sm_step, 1)
                    eng.wait_ge(sm_step, SM * a + 8)
                    wait(eng, mix_done, i - 1)
                    for b in range(2):
                        s = eng.tensor_tensor(attn[:, b, :].rearrange("p (h e) -> p h e", h=HEADS),
                                              probs[:, b, :].unsqueeze(1).broadcast_to([C, HEADS, D]),
                                              const("head", C).rearrange("p (h e) -> p h e", h=HEADS), ALU.mult)
                    s.then_inc(attn_ready, 1)
                if last_heads(i):
                    gate_present(0)
                    gate_scores(0)
                if conv:
                    taps(i, par, 3, 5)
                if i_is(i, PAIRS - 1):
                    gate_compare(0)
                if conv:
                    taps(i, par, 5, 6)
                if att:
                    eng.wait_ge(out_done, i)
                    eng.tensor_tensor(x_sb[:, a, :], x_sb[:, a, :], out_ps[0:C, :], ALU.add).then_inc(x1_done, 1)
                    x1_stats(a)
                if moe:
                    eng.wait_ge(gate_done, i - 1)
                    eng.scalar_tensor_tensor(
                        out=logits[:, m, :, :],
                        in0=small_ps[:, LOGIT:LOGIT + 4 * TILES].rearrange("p (t e) -> p t e", t=TILES),
                        scalar=1.0 / X_SCALE, in1=gate_b_sb[:, :].unsqueeze(1).broadcast_to([128, TILES, EXPERTS]),
                        op0=ALU.mult, op1=ALU.add).then_inc(logit_free, 1)
                if ahead or att:
                    channel_means(i + 1, ahead, att)
                if last_heads(i):
                    gate_weights(0)

            SM = 8
            OUTER = [(dy, dx) for dy in (-1, 0, 1) for dx in (-1, 0, 1) if (dy, dx) != (0, 0)]

            def taps(i, par, lo, hi):
                if lo == 0:
                    eng.wait_ge(v_init, i + 1)
                for n in range(lo, hi):
                    dy, dx = OUTER[n]
                    t = 3 * (dy + 1) + dx + 1
                    wait(eng, tap_done, 8 * i + n)
                    eng.scalar_tensor_tensor(out=v_acc[par][:, :, :], in0=v_window(dy, dx), scalar=v_taps[:, t:t + 1],
                                             in1=v_acc[par][:, :, :], op0=ALU.mult, op1=ALU.add).then_inc(tap_done, 1)

            eng.wait_ge(in_x[0], 16)
            x_stats(0)
            eng.wait_ge(ones_set, 1)
            channel_means(-1, True, False)
            turns(eng, turn)

            gate_logits(1)
            gate_compare(1)
            gate_beaten(eng, 1)
            gate_rank(1)
            gate_present(1)
            eng.wait_ge(count_done, 1)
            eng.tensor_scalar(on_rows[:, :], small_ps[0:U, 0:2 * EXPERTS], 1.0, None, ALU.min)
            eng.tensor_scalar(on_cols[:, :], small_ps[0:EXPERTS, 16:16 + U], 1.0, None, ALU.min)\
               .then_inc(on_cols_ready, 1)
            eng.wait_ge(on_cols_ready, 1)
            step(eng.tensor_scalar(spread0[:, :], on_rows[:, 0:EXPERTS], const("sel", U)[:, 0:1], None, ALU.mult))
            step(eng.scalar_tensor_tensor(out=spread1[:, :], in0=on_rows[:, EXPERTS:2 * EXPERTS],
                                          scalar=const("sel", U)[:, 1:2], in1=spread0[:, :],
                                          op0=ALU.mult, op1=ALU.add))
            eng.tensor_copy(spread[:, :].rearrange("p (e d) -> p e d", e=EXPERTS),
                            spread1[:, :].unsqueeze(2).broadcast_to([U, EXPERTS, C])).then_inc(spread_ready, 1)

            def mix(i, par):
                wait(eng, y_done, i - 1)
                for m in range(MT):
                    eng.wait_ge(coef_done, MT * i + m + 1)
                    eng.tensor_tensor(h_mixed[par][:, m, :], hidden[:, i, m, :], bank[m][:, :], ALU.mult)\
                       .then_inc(mixed_done, 1)

            def add(i, par):
                eng.wait_ge(y_done, i + 1)
                wait(eng, stored[par], 8 * (i - par))
                eng.tensor_tensor(out_sb[par][:, :], x_sb[:, i, :], y_ps[par][0:C, :], ALU.add)\
                   .then_inc(y_taken, 1)

            mix(0, 0)
            gate_scores(1)
            mix(1, 1)
            gate_weights(1)
            gate_parts(1)
            add(0, 0)
            mix(2, 0)
            add(1, 1)
            with eng.Fori(1, PAIRS // 2 - 1) as k:
                mix(2 * k + 1, 1)
                add(2 * k, 0)
                mix(2 * k + 2, 0)
                add(2 * k + 1, 1)
            eng.wait_ge(hid_free, MT * PAIRS + 3)
            mix(PAIRS - 1, 1)
            add(PAIRS - 2, 0)
            for b in range(2):
                t = slice(b * HW, (b + 1) * HW)
                eng.wait_ge(y_done, PAIRS + b)
                eng.wait_ge(stored[1], 8 * (PAIRS - 2))
                eng.tensor_tensor(out_sb[1][:, t], x_sb[:, PAIRS - 1, t], y_ps[1 - b][0:C, t], ALU.add)\
                   .then_inc(y_taken, 1)


def constants():
    import numpy as np
    c = np.arange(C)
    t = {n: np.zeros((128, w), np.float32) for n, w in CONSTS}
    t["ident"][:] = np.eye(128)
    same = (c[:, None] // GROUP == c[None, :] // GROUP) / GROUP
    t["avg"][:C] = same
    t["dev"][:C] = np.eye(C) - same
    t["head"][:C] = c[:, None] // D == c[None, :] // D
    t["slot"][:C] = c[:, None] % D == np.arange(D)[None, :]
    e = np.arange(EXPERTS)
    t["tri"][:] = (e[None, :] < e[:, None]).reshape(1, 16)
    bias_part = [0, 1, 2, 0, 1, 0]
    for k in range(U):
        t["sel"][k, k // URANK] = bias_part[k % URANK] == 0
        t["part"][k, bias_part[k % URANK]] = 1.0
    return np.concatenate([t[n] for n, _ in CONSTS], axis=1)


_INS = ["x", "L0_conv_w_qkv", "L0_conv_w_dw", "L0_conv_w_proj", "L0_conv_temperature", "L1_conv_gate_w",
        "L1_conv_gate_b", "L1_conv_w1", "L1_conv_b1", "L1_conv_w2", "L1_conv_b2"]


def kernel(**inputs):
    import numpy as np
    import concourse.bacc as bacc
    from concourse.bass_utils import run_bass_kernel_spmd

    nc = bacc.Bacc("TRN2", target_bir_lowering=False, num_devices=1)
    arrays, args = {}, []
    named = [(n, np.ascontiguousarray(inputs[n])) for n in _INS] + [("consts", constants())]
    for name, a in named:
        arrays[f"in_{name}"] = a
        args.append(nc.dram_tensor(f"in_{name}", a.shape, mybir.dt.from_np(a.dtype), kind="ExternalInput").ap())
    out = nc.dram_tensor("out_0", (B, C, H, W), F32, kind="ExternalOutput").ap()
    build(nc, *args, out)
    r = run_bass_kernel_spmd(nc, [arrays], core_ids=[0])
    return r.results[0]["out_0"]
```
